# Optimizing a Trainium2 kernel written in Bass

```python
import numpy as np
import jax
import jax.numpy as jnp

def _softmax(x, axis=-1):
    return jax.nn.softmax(x, axis=axis)

def _gelu(x):
    return jax.nn.gelu(x, approximate=True)

def _silu(x):
    return jax.nn.silu(x)

def _sigmoid(x):
    return jax.nn.sigmoid(x)

def _layernorm(x, axis=-1, eps=1e-05):
    m = jnp.mean(x, axis=axis, keepdims=True)
    v = jnp.var(x, axis=axis, keepdims=True)
    return (x - m) / jnp.sqrt(v + eps)

def _scatter_add(tgt, idx, src, axis=0):
    return tgt.at[idx].add(src)

def _segment_sum(src, seg, n):
    return jax.ops.segment_sum(src, seg, n)
kernel_name = 'mk_xattn_seq_d4_seqx_r8_c1f85d'

def setup_inputs(seed: int=0):
    np.random.seed(seed)
    _w = jnp.asarray

    def _rec_inputs():
        import jax
        import jax.numpy as jnp
        _rk = jax.random.key(seed)
        x = 7.22e-05 + 1 * jax.random.normal(jax.random.fold_in(_rk, 1), (32, 64, 256), jnp.float32)
        _lenS = 64 - jax.random.randint(jax.random.fold_in(_rk, 7), (32,), 0, max(1, 64 // 4) + 1, jnp.int32)
        _lenS2 = 64 - jax.random.randint(jax.random.fold_in(_rk, 8), (32,), 0, max(1, 64 // 4) + 1, jnp.int32)
        _ctx_2048P = jax.random.normal(jax.random.fold_in(_rk, 11), (32, 16, 256), jnp.float32)
        _ctx_2048c = jax.random.dirichlet(jax.random.fold_in(_rk, 511), 0.3 * jnp.ones((16,), jnp.float32), (32, 64))
        _ctx_2048t = jnp.einsum('bsk,bkd->bsd', _ctx_2048c, _ctx_2048P)
        _ctx_2048t = _ctx_2048t * jax.lax.rsqrt(jnp.mean(jnp.square(_ctx_2048t)) + 1e-12) * 0.953939
        ctx_2048 = 3.03215e-05 + 0.0999827 * (_ctx_2048t + 0.3 * jax.random.normal(jax.random.fold_in(_rk, 611), (32, 64, 256), jnp.float32))
        _validS = jnp.arange(64)[None, :] < _lenS[:, None]
        _validS2 = jnp.arange(64)[None, :] < _lenS2[:, None]
        _causal = jnp.tril(jnp.ones((64, 64), dtype=bool))
        mask_BxS2_bf1 = jnp.ones((32, 64), dtype=bool)
        return (x, ctx_2048, mask_BxS2_bf1)
    x, ctx_2048, mask_BxS2_bf1 = _rec_inputs()

    def _L0_xattn_setup():
        import jax, jax.numpy as jnp
        import numpy as np
        N_HEAD = 32
        EPS = 1e-05

        def _ln(x, w, b):
            m = jnp.mean(x, axis=-1, keepdims=True)
            v = jnp.mean((x - m) ** 2, axis=-1, keepdims=True)
            return (x - m) * jax.lax.rsqrt(v + EPS) * w + b

        def _forward(x, state, i, ln1_w, ln1_b, ln2_w, ln2_b, maa_x, maa_w, maa_k, maa_v, maa_r, maa_g, maa_w1, maa_w2, time_decay, decay_w1, decay_w2, faaaa, Wr, Wk, Wv, Wg, Wo, gn_w, gn_b, fmaa_k, fmaa_r, fWk, fWr, fWv):
            B, L, C = x.shape
            H = N_HEAD
            S = C // H
            i0 = (2 + S) * i
            xa = _ln(x, ln1_w, ln1_b)
            sx = jnp.concatenate([state[:, i0 + 1][:, None], xa[:, :-1]], axis=1) - xa
            xxx = xa + sx * maa_x
            t = jnp.tanh(xxx @ maa_w1).reshape(B, L, 5, -1)
            m = jnp.einsum('blfd,fdc->blfc', t, maa_w2)
            mw, mk, mv, mr, mg = (m[:, :, j] for j in range(5))
            xw = xa + sx * (maa_w + mw)
            xk = xa + sx * (maa_k + mk)
            xv = xa + sx * (maa_v + mv)
            xr = xa + sx * (maa_r + mr)
            xg = xa + sx * (maa_g + mg)
            w = time_decay + jnp.tanh(xw @ decay_w1) @ decay_w2
            w = jnp.exp(-jnp.exp(w)).reshape(B, L, H, S)
            r = (xr @ Wr.T).reshape(B, L, H, S)
            k = (xk @ Wk.T).reshape(B, L, H, S)
            v = (xv @ Wv.T).reshape(B, L, H, S)
            g = jax.nn.silu(xg @ Wg.T)
            s0 = state[:, i0 + 2:i0 + 2 + S].reshape(B, H, S, S)

            def step(s, inp):
                k_l, v_l, w_l, r_l = inp
                a = k_l[..., :, None] * v_l[..., None, :]
                out = jnp.einsum('bhs,bhst->bht', r_l, faaaa * a + s)
                s_new = a + w_l[..., None] * s
                return (s_new, out)
            seq = tuple((z.transpose(1, 0, 2, 3) for z in (k, v, w, r)))
            _, outs = jax.lax.scan(step, s0, seq)
            y = outs.transpose(1, 0, 2, 3)
            gm = jnp.mean(y, axis=-1, keepdims=True)
            gv = jnp.mean((y - gm) ** 2, axis=-1, keepdims=True)
            y = ((y - gm) * jax.lax.rsqrt(gv + EPS)).reshape(B, L, C) * gn_w + gn_b
            x = x + y * g @ Wo.T
            xc = _ln(x, ln2_w, ln2_b)
            sxc = jnp.concatenate([state[:, i0][:, None], xc[:, :-1]], axis=1) - xc
            xk2 = xc + sxc * fmaa_k
            xr2 = xc + sxc * fmaa_r
            rr = jax.nn.sigmoid(xr2 @ fWr.T)
            kk = jnp.square(jax.nn.relu(xk2 @ fWk.T))
            x = x + rr * (kk @ fWv.T)
            return x
        key = jax.random.key(seed)
        B, L, C, H = (8, 64, 256, N_HEAD)
        S = C // H
        DM, DD = (32, 64)
        ks = jax.random.split(key, 32)
        n = lambda k, shp, s=1.0: jax.random.normal(k, shp, dtype=jnp.float32) * s
        u = lambda k, shp: jax.random.uniform(k, shp, dtype=jnp.float32)
        inp = {'x': n(ks[0], (B, L, C)), 'state': n(ks[1], (B, 2 + S, C), 0.1), 'i': 0, 'ln1_w': jnp.ones((C,), jnp.float32), 'ln1_b': jnp.zeros((C,), jnp.float32), 'ln2_w': jnp.ones((C,), jnp.float32), 'ln2_b': jnp.zeros((C,), jnp.float32), 'maa_x': u(ks[2], (C,)), 'maa_w': u(ks[3], (C,)), 'maa_k': u(ks[4], (C,)), 'maa_v': u(ks[5], (C,)), 'maa_r': u(ks[6], (C,)), 'maa_g': u(ks[7], (C,)), 'maa_w1': n(ks[8], (C, 5 * DM), 0.02), 'maa_w2': n(ks[9], (5, DM, C), 0.02), 'time_decay': n(ks[10], (C,), 0.5), 'decay_w1': n(ks[11], (C, DD), 0.02), 'decay_w2': n(ks[12], (DD, C), 0.02), 'faaaa': n(ks[13], (H, S, 1), 0.1), 'Wr': n(ks[14], (C, C), 0.02), 'Wk': n(ks[15], (C, C), 0.02), 'Wv': n(ks[16], (C, C), 0.02), 'Wg': n(ks[17], (C, C), 0.02), 'Wo': n(ks[18], (C, C), 0.02), 'gn_w': jnp.ones((C,), jnp.float32), 'gn_b': jnp.zeros((C,), jnp.float32), 'fmaa_k': u(ks[19], (C,)), 'fmaa_r': u(ks[20], (C,)), 'fWk': n(ks[21], (C, C), 0.02), 'fWr': n(ks[22], (C, C), 0.02), 'fWv': n(ks[23], (C, C), 0.02)}
        return inp
    _L0_xattn_all = _L0_xattn_setup()
    _L0_xattn_in = {k: v for k, v in _L0_xattn_all.items() if k in ('ln1_w', 'ln1_b', 'ln2_w', 'ln2_b', 'maa_x', 'maa_w', 'maa_k', 'maa_v', 'maa_r', 'maa_g', 'maa_w1', 'maa_w2', 'time_decay', 'decay_w1', 'decay_w2', 'faaaa', 'Wr', 'Wk', 'Wv', 'Wg', 'Wo', 'gn_w', 'gn_b', 'fmaa_k', 'fmaa_r', 'fWk', 'fWr', 'fWv')}
    del _L0_xattn_all

    def _L1_xattn_setup():
        import jax, jax.numpy as jnp
        import numpy as np
        E, H, L, B = (256, 32, 128, 4)
        S = E // H
        DM, DD = (32, 64)

        def _ln(x, w, b, eps=1e-05):
            m = x.mean(-1, keepdims=True)
            v = ((x - m) ** 2).mean(-1, keepdims=True)
            return (x - m) / jnp.sqrt(v + eps) * w + b

        def _block(x, state, ln1_w, ln1_b, ln2_w, ln2_b, maa_x, maa_w1, maa_w2, maa_stack, time_decay, td_w1, td_w2, u, Wr, Wk, Wv, Wg, Wo, gn_w, gn_b, ffn_maa_k, ffn_maa_r, Wfk, Wfr, Wfv):
            b, l, e = x.shape
            h = u.shape[0]
            s_ = e // h
            xa = _ln(x, ln1_w, ln1_b)
            sx = jnp.concatenate([state[:, 1:2] - xa[:, :1], xa[:, :-1] - xa[:, 1:]], axis=1)
            xxx = jnp.tanh((xa + sx * maa_x) @ maa_w1).reshape(b, l, 5, DM)
            xxx = jnp.einsum('blfd,fde->blfe', xxx, maa_w2)
            xm = xa[:, :, None] + sx[:, :, None] * (maa_stack + xxx)
            xk, xw, xv, xr, xg = (xm[:, :, j] for j in range(5))
            w = jnp.exp(-jnp.exp(time_decay + jnp.tanh(xw @ td_w1) @ td_w2)).reshape(b, l, h, s_)
            r = (xr @ Wr.T).reshape(b, l, h, s_)
            k = (xk @ Wk.T).reshape(b, l, h, s_)
            v = (xv @ Wv.T).reshape(b, l, h, s_)
            g = jax.nn.silu(xg @ Wg.T)
            s0 = state[:, 2:2 + s_].reshape(b, h, s_, s_)

            def step(s, rkvw):
                r_t, k_t, v_t, w_t = rkvw
                a = k_t[..., :, None] * v_t[..., None, :]
                out = jnp.einsum('bhi,bhij->bhj', r_t, u * a + s)
                s = a + w_t[..., :, None] * s
                return (s, out)
            rkvw = tuple((jnp.moveaxis(t, 1, 0) for t in (r, k, v, w)))
            _, out = jax.lax.scan(step, s0, rkvw)
            out = jnp.moveaxis(out, 0, 1).reshape(b, l, e)
            og = out.reshape(b, l, h, s_)
            m = og.mean(-1, keepdims=True)
            va = ((og - m) ** 2).mean(-1, keepdims=True)
            og = ((og - m) / jnp.sqrt(va + 1e-05)).reshape(b, l, e) * gn_w + gn_b
            x1 = x + og * g @ Wo.T
            xc = _ln(x1, ln2_w, ln2_b)
            sx2 = jnp.concatenate([state[:, 0:1] - xc[:, :1], xc[:, :-1] - xc[:, 1:]], axis=1)
            xk2 = xc + sx2 * ffn_maa_k
            xr2 = xc + sx2 * ffn_maa_r
            rr = jax.nn.sigmoid(xr2 @ Wfr.T)
            kk = jnp.square(jax.nn.relu(xk2 @ Wfk.T))
            return x1 + rr * (kk @ Wfv.T)
        key = jax.random.key(seed)
        ks = jax.random.split(key, 24)
        sc = 0.02
        d = {'x': jax.random.normal(ks[0], (B, L, E), jnp.float32), 'state': jax.random.normal(ks[1], (B, 2 + S, E), jnp.float32) * 0.1, 'ln1_w': jnp.ones((E,), jnp.float32), 'ln1_b': jnp.zeros((E,), jnp.float32), 'ln2_w': jnp.ones((E,), jnp.float32), 'ln2_b': jnp.zeros((E,), jnp.float32), 'maa_x': jax.random.normal(ks[2], (E,), jnp.float32) * 0.1, 'maa_w1': jax.random.normal(ks[3], (E, 5 * DM), jnp.float32) * sc, 'maa_w2': jax.random.normal(ks[4], (5, DM, E), jnp.float32) * sc, 'maa_stack': jax.random.normal(ks[5], (1, 5, E), jnp.float32) * 0.1, 'time_decay': jax.random.normal(ks[6], (E,), jnp.float32) * 0.5, 'td_w1': jax.random.normal(ks[7], (E, DD), jnp.float32) * sc, 'td_w2': jax.random.normal(ks[8], (DD, E), jnp.float32) * sc, 'u': jax.random.normal(ks[9], (H, S, 1), jnp.float32) * 0.1, 'Wr': jax.random.normal(ks[10], (E, E), jnp.float32) * sc, 'Wk': jax.random.normal(ks[11], (E, E), jnp.float32) * sc, 'Wv': jax.random.normal(ks[12], (E, E), jnp.float32) * sc, 'Wg': jax.random.normal(ks[13], (E, E), jnp.float32) * sc, 'Wo': jax.random.normal(ks[14], (E, E), jnp.float32) * sc, 'gn_w': jnp.ones((E,), jnp.float32), 'gn_b': jnp.zeros((E,), jnp.float32), 'ffn_maa_k': jax.random.normal(ks[15], (E,), jnp.float32) * 0.1, 'ffn_maa_r': jax.random.normal(ks[16], (E,), jnp.float32) * 0.1, 'Wfk': jax.random.normal(ks[17], (E, E), jnp.float32) * sc, 'Wfr': jax.random.normal(ks[18], (E, E), jnp.float32) * sc, 'Wfv': jax.random.normal(ks[19], (E, E), jnp.float32) * sc}
        return d
    _L1_xattn_all = _L1_xattn_setup()
    _L1_xattn_in = {k: v for k, v in _L1_xattn_all.items() if k in ('ln1_w', 'ln1_b', 'ln2_w', 'ln2_b', 'maa_x', 'maa_w1', 'maa_w2', 'maa_stack', 'time_decay', 'td_w1', 'td_w2', 'u', 'Wr', 'Wk', 'Wv', 'Wg', 'Wo', 'gn_w', 'gn_b', 'ffn_maa_k', 'ffn_maa_r', 'Wfk', 'Wfr', 'Wfv')}
    del _L1_xattn_all

    def _L2_xattn_setup():
        import jax, jax.numpy as jnp
        import numpy as np
        B, C, CI, T = (8, 64, 32, 256)
        EPS = 1e-05
        key = jax.random.key(seed)
        ks = jax.random.split(key, 8)
        inv_c = 1.0 / np.sqrt(C)
        inv_ci = 1.0 / np.sqrt(CI)
        return {'x_this': jax.random.normal(ks[0], (B, C, T), jnp.float32), 'x_other': jax.random.normal(ks[1], (B, C, T), jnp.float32), 'Wg': jax.random.normal(ks[2], (CI, C), jnp.float32) * inv_c, 'bg': jnp.zeros((CI,), jnp.float32), 'Wtheta': jax.random.normal(ks[3], (CI, C), jnp.float32) * inv_c, 'btheta': jnp.zeros((CI,), jnp.float32), 'Wphi': jax.random.normal(ks[4], (CI, C), jnp.float32) * inv_c, 'bphi': jnp.zeros((CI,), jnp.float32), 'Wz': jax.random.normal(ks[5], (C, CI), jnp.float32) * inv_ci, 'bz': jnp.zeros((C,), jnp.float32), 'gamma': jax.random.normal(ks[6], (C,), jnp.float32), 'beta': jax.random.normal(ks[7], (C,), jnp.float32)}
    _L2_xattn_all = _L2_xattn_setup()
    _L2_xattn_in = {k: v for k, v in _L2_xattn_all.items() if k in ('Wg', 'bg', 'Wtheta', 'btheta', 'Wphi', 'bphi', 'Wz', 'bz', 'gamma', 'beta')}
    del _L2_xattn_all

    def _L3_xattn_setup():
        import jax, jax.numpy as jnp
        import numpy as np
        HIDDEN = 256
        HEADS = 16
        HEAD_DIM = HIDDEN // HEADS
        LN_EPS = 1e-05
        GATE_INIT = 0.5

        def _layer_norm(x, gamma, beta):
            mu = jnp.mean(x, axis=-1, keepdims=True)
            var = jnp.mean(jnp.square(x - mu), axis=-1, keepdims=True)
            return (x - mu) * jax.lax.rsqrt(var + LN_EPS) * gamma + beta
        key = jax.random.key(seed)
        ks = jax.random.split(key, 8)
        B, T_TEXT, T_AUDIO = (4, 256, 1500)
        s = 0.02
        return {'hidden_states': jax.random.normal(ks[0], (B, T_TEXT, HIDDEN), jnp.float32), 'audio_kv': jax.random.normal(ks[1], (B, T_AUDIO, HIDDEN), jnp.float32), 'audio_attention_mask': jnp.ones((B, T_AUDIO), dtype=bool), 'Wq': jax.random.normal(ks[2], (HIDDEN, HIDDEN), jnp.float32) * s, 'Wk': jax.random.normal(ks[3], (HIDDEN, HIDDEN), jnp.float32) * s, 'Wv': jax.random.normal(ks[4], (HIDDEN, HIDDEN), jnp.float32) * s, 'Wo': jax.random.normal(ks[5], (HIDDEN, HIDDEN), jnp.float32) * s, 'ln_gamma': jnp.ones((HIDDEN,), jnp.float32), 'ln_beta': jnp.zeros((HIDDEN,), jnp.float32), 'gate': jnp.array([GATE_INIT], jnp.float32)}
    _L3_xattn_all = _L3_xattn_setup()
    _L3_xattn_in = {k: v for k, v in _L3_xattn_all.items() if k in ('Wq', 'Wk', 'Wv', 'Wo', 'ln_gamma', 'ln_beta', 'gate')}
    del _L3_xattn_all
    return {'x': x, 'ctx_2048': ctx_2048, 'mask_BxS2_bf1': mask_BxS2_bf1, 'L0_xattn_ln1_w': _L0_xattn_in['ln1_w'], 'L0_xattn_ln1_b': _L0_xattn_in['ln1_b'], 'L0_xattn_ln2_w': _L0_xattn_in['ln2_w'], 'L0_xattn_ln2_b': _L0_xattn_in['ln2_b'], 'L0_xattn_maa_x': _L0_xattn_in['maa_x'], 'L0_xattn_maa_w': _L0_xattn_in['maa_w'], 'L0_xattn_maa_k': _L0_xattn_in['maa_k'], 'L0_xattn_maa_v': _L0_xattn_in['maa_v'], 'L0_xattn_maa_r': _L0_xattn_in['maa_r'], 'L0_xattn_maa_g': _L0_xattn_in['maa_g'], 'L0_xattn_maa_w1': _L0_xattn_in['maa_w1'], 'L0_xattn_maa_w2': _L0_xattn_in['maa_w2'], 'L0_xattn_time_decay': _L0_xattn_in['time_decay'], 'L0_xattn_decay_w1': _L0_xattn_in['decay_w1'], 'L0_xattn_decay_w2': _L0_xattn_in['decay_w2'], 'L0_xattn_faaaa': _L0_xattn_in['faaaa'], 'L0_xattn_Wr': _L0_xattn_in['Wr'], 'L0_xattn_Wk': _L0_xattn_in['Wk'], 'L0_xattn_Wv': _L0_xattn_in['Wv'], 'L0_xattn_Wg': _L0_xattn_in['Wg'], 'L0_xattn_Wo': _L0_xattn_in['Wo'], 'L0_xattn_gn_w': _L0_xattn_in['gn_w'], 'L0_xattn_gn_b': _L0_xattn_in['gn_b'], 'L0_xattn_fmaa_k': _L0_xattn_in['fmaa_k'], 'L0_xattn_fmaa_r': _L0_xattn_in['fmaa_r'], 'L0_xattn_fWk': _L0_xattn_in['fWk'], 'L0_xattn_fWr': _L0_xattn_in['fWr'], 'L0_xattn_fWv': _L0_xattn_in['fWv'], 'L1_xattn_ln1_w': _L1_xattn_in['ln1_w'], 'L1_xattn_ln1_b': _L1_xattn_in['ln1_b'], 'L1_xattn_ln2_w': _L1_xattn_in['ln2_w'], 'L1_xattn_ln2_b': _L1_xattn_in['ln2_b'], 'L1_xattn_maa_x': _L1_xattn_in['maa_x'], 'L1_xattn_maa_w1': _L1_xattn_in['maa_w1'], 'L1_xattn_maa_w2': _L1_xattn_in['maa_w2'], 'L1_xattn_maa_stack': _L1_xattn_in['maa_stack'], 'L1_xattn_time_decay': _L1_xattn_in['time_decay'], 'L1_xattn_td_w1': _L1_xattn_in['td_w1'], 'L1_xattn_td_w2': _L1_xattn_in['td_w2'], 'L1_xattn_u': _L1_xattn_in['u'], 'L1_xattn_Wr': _L1_xattn_in['Wr'], 'L1_xattn_Wk': _L1_xattn_in['Wk'], 'L1_xattn_Wv': _L1_xattn_in['Wv'], 'L1_xattn_Wg': _L1_xattn_in['Wg'], 'L1_xattn_Wo': _L1_xattn_in['Wo'], 'L1_xattn_gn_w': _L1_xattn_in['gn_w'], 'L1_xattn_gn_b': _L1_xattn_in['gn_b'], 'L1_xattn_ffn_maa_k': _L1_xattn_in['ffn_maa_k'], 'L1_xattn_ffn_maa_r': _L1_xattn_in['ffn_maa_r'], 'L1_xattn_Wfk': _L1_xattn_in['Wfk'], 'L1_xattn_Wfr': _L1_xattn_in['Wfr'], 'L1_xattn_Wfv': _L1_xattn_in['Wfv'], 'L2_xattn_Wg': _L2_xattn_in['Wg'], 'L2_xattn_bg': _L2_xattn_in['bg'], 'L2_xattn_Wtheta': _L2_xattn_in['Wtheta'], 'L2_xattn_btheta': _L2_xattn_in['btheta'], 'L2_xattn_Wphi': _L2_xattn_in['Wphi'], 'L2_xattn_bphi': _L2_xattn_in['bphi'], 'L2_xattn_Wz': _L2_xattn_in['Wz'], 'L2_xattn_bz': _L2_xattn_in['bz'], 'L2_xattn_gamma': _L2_xattn_in['gamma'], 'L2_xattn_beta': _L2_xattn_in['beta'], 'L3_xattn_Wq': _L3_xattn_in['Wq'], 'L3_xattn_Wk': _L3_xattn_in['Wk'], 'L3_xattn_Wv': _L3_xattn_in['Wv'], 'L3_xattn_Wo': _L3_xattn_in['Wo'], 'L3_xattn_ln_gamma': _L3_xattn_in['ln_gamma'], 'L3_xattn_ln_beta': _L3_xattn_in['ln_beta'], 'L3_xattn_gate': _L3_xattn_in['gate']}

def reference(x, ctx_2048, mask_BxS2_bf1, L0_xattn_ln1_w, L0_xattn_ln1_b, L0_xattn_ln2_w, L0_xattn_ln2_b, L0_xattn_maa_x, L0_xattn_maa_w, L0_xattn_maa_k, L0_xattn_maa_v, L0_xattn_maa_r, L0_xattn_maa_g, L0_xattn_maa_w1, L0_xattn_maa_w2, L0_xattn_time_decay, L0_xattn_decay_w1, L0_xattn_decay_w2, L0_xattn_faaaa, L0_xattn_Wr, L0_xattn_Wk, L0_xattn_Wv, L0_xattn_Wg, L0_xattn_Wo, L0_xattn_gn_w, L0_xattn_gn_b, L0_xattn_fmaa_k, L0_xattn_fmaa_r, L0_xattn_fWk, L0_xattn_fWr, L0_xattn_fWv, L1_xattn_ln1_w, L1_xattn_ln1_b, L1_xattn_ln2_w, L1_xattn_ln2_b, L1_xattn_maa_x, L1_xattn_maa_w1, L1_xattn_maa_w2, L1_xattn_maa_stack, L1_xattn_time_decay, L1_xattn_td_w1, L1_xattn_td_w2, L1_xattn_u, L1_xattn_Wr, L1_xattn_Wk, L1_xattn_Wv, L1_xattn_Wg, L1_xattn_Wo, L1_xattn_gn_w, L1_xattn_gn_b, L1_xattn_ffn_maa_k, L1_xattn_ffn_maa_r, L1_xattn_Wfk, L1_xattn_Wfr, L1_xattn_Wfv, L2_xattn_Wg, L2_xattn_bg, L2_xattn_Wtheta, L2_xattn_btheta, L2_xattn_Wphi, L2_xattn_bphi, L2_xattn_Wz, L2_xattn_bz, L2_xattn_gamma, L2_xattn_beta, L3_xattn_Wq, L3_xattn_Wk, L3_xattn_Wv, L3_xattn_Wo, L3_xattn_ln_gamma, L3_xattn_ln_beta, L3_xattn_gate):
    import jax
    import jax.numpy as jnp

    def _L0_xattn_ref(x, state, i, ln1_w, ln1_b, ln2_w, ln2_b, maa_x, maa_w, maa_k, maa_v, maa_r, maa_g, maa_w1, maa_w2, time_decay, decay_w1, decay_w2, faaaa, Wr, Wk, Wv, Wg, Wo, gn_w, gn_b, fmaa_k, fmaa_r, fWk, fWr, fWv):
        import jax, jax.numpy as jnp
        import numpy as np
        N_HEAD = 32
        EPS = 1e-05

        def _ln(x, w, b):
            m = jnp.mean(x, axis=-1, keepdims=True)
            v = jnp.mean((x - m) ** 2, axis=-1, keepdims=True)
            return (x - m) * jax.lax.rsqrt(v + EPS) * w + b

        def _forward(x, state, i, ln1_w, ln1_b, ln2_w, ln2_b, maa_x, maa_w, maa_k, maa_v, maa_r, maa_g, maa_w1, maa_w2, time_decay, decay_w1, decay_w2, faaaa, Wr, Wk, Wv, Wg, Wo, gn_w, gn_b, fmaa_k, fmaa_r, fWk, fWr, fWv):
            B, L, C = x.shape
            H = N_HEAD
            S = C // H
            i0 = (2 + S) * i
            xa = _ln(x, ln1_w, ln1_b)
            sx = jnp.concatenate([state[:, i0 + 1][:, None], xa[:, :-1]], axis=1) - xa
            xxx = xa + sx * maa_x
            t = jnp.tanh(xxx @ maa_w1).reshape(B, L, 5, -1)
            m = jnp.einsum('blfd,fdc->blfc', t, maa_w2)
            mw, mk, mv, mr, mg = (m[:, :, j] for j in range(5))
            xw = xa + sx * (maa_w + mw)
            xk = xa + sx * (maa_k + mk)
            xv = xa + sx * (maa_v + mv)
            xr = xa + sx * (maa_r + mr)
            xg = xa + sx * (maa_g + mg)
            w = time_decay + jnp.tanh(xw @ decay_w1) @ decay_w2
            w = jnp.exp(-jnp.exp(w)).reshape(B, L, H, S)
            r = (xr @ Wr.T).reshape(B, L, H, S)
            k = (xk @ Wk.T).reshape(B, L, H, S)
            v = (xv @ Wv.T).reshape(B, L, H, S)
            g = jax.nn.silu(xg @ Wg.T)
            s0 = state[:, i0 + 2:i0 + 2 + S].reshape(B, H, S, S)

            def step(s, inp):
                k_l, v_l, w_l, r_l = inp
                a = k_l[..., :, None] * v_l[..., None, :]
                out = jnp.einsum('bhs,bhst->bht', r_l, faaaa * a + s)
                s_new = a + w_l[..., None] * s
                return (s_new, out)
            seq = tuple((z.transpose(1, 0, 2, 3) for z in (k, v, w, r)))
            _, outs = jax.lax.scan(step, s0, seq)
            y = outs.transpose(1, 0, 2, 3)
            gm = jnp.mean(y, axis=-1, keepdims=True)
            gv = jnp.mean((y - gm) ** 2, axis=-1, keepdims=True)
            y = ((y - gm) * jax.lax.rsqrt(gv + EPS)).reshape(B, L, C) * gn_w + gn_b
            x = x + y * g @ Wo.T
            xc = _ln(x, ln2_w, ln2_b)
            sxc = jnp.concatenate([state[:, i0][:, None], xc[:, :-1]], axis=1) - xc
            xk2 = xc + sxc * fmaa_k
            xr2 = xc + sxc * fmaa_r
            rr = jax.nn.sigmoid(xr2 @ fWr.T)
            kk = jnp.square(jax.nn.relu(xk2 @ fWk.T))
            x = x + rr * (kk @ fWv.T)
            return x
        return _forward(x, state, i, ln1_w, ln1_b, ln2_w, ln2_b, maa_x, maa_w, maa_k, maa_v, maa_r, maa_g, maa_w1, maa_w2, time_decay, decay_w1, decay_w2, faaaa, Wr, Wk, Wv, Wg, Wo, gn_w, gn_b, fmaa_k, fmaa_r, fWk, fWr, fWv)

    def _L1_xattn_ref(x, state, ln1_w, ln1_b, ln2_w, ln2_b, maa_x, maa_w1, maa_w2, maa_stack, time_decay, td_w1, td_w2, u, Wr, Wk, Wv, Wg, Wo, gn_w, gn_b, ffn_maa_k, ffn_maa_r, Wfk, Wfr, Wfv):
        import jax, jax.numpy as jnp
        import numpy as np
        E, H, L, B = (256, 32, 128, 4)
        S = E // H
        DM, DD = (32, 64)

        def _ln(x, w, b, eps=1e-05):
            m = x.mean(-1, keepdims=True)
            v = ((x - m) ** 2).mean(-1, keepdims=True)
            return (x - m) / jnp.sqrt(v + eps) * w + b

        def _block(x, state, ln1_w, ln1_b, ln2_w, ln2_b, maa_x, maa_w1, maa_w2, maa_stack, time_decay, td_w1, td_w2, u, Wr, Wk, Wv, Wg, Wo, gn_w, gn_b, ffn_maa_k, ffn_maa_r, Wfk, Wfr, Wfv):
            b, l, e = x.shape
            h = u.shape[0]
            s_ = e // h
            xa = _ln(x, ln1_w, ln1_b)
            sx = jnp.concatenate([state[:, 1:2] - xa[:, :1], xa[:, :-1] - xa[:, 1:]], axis=1)
            xxx = jnp.tanh((xa + sx * maa_x) @ maa_w1).reshape(b, l, 5, DM)
            xxx = jnp.einsum('blfd,fde->blfe', xxx, maa_w2)
            xm = xa[:, :, None] + sx[:, :, None] * (maa_stack + xxx)
            xk, xw, xv, xr, xg = (xm[:, :, j] for j in range(5))
            w = jnp.exp(-jnp.exp(time_decay + jnp.tanh(xw @ td_w1) @ td_w2)).reshape(b, l, h, s_)
            r = (xr @ Wr.T).reshape(b, l, h, s_)
            k = (xk @ Wk.T).reshape(b, l, h, s_)
            v = (xv @ Wv.T).reshape(b, l, h, s_)
            g = jax.nn.silu(xg @ Wg.T)
            s0 = state[:, 2:2 + s_].reshape(b, h, s_, s_)

            def step(s, rkvw):
                r_t, k_t, v_t, w_t = rkvw
                a = k_t[..., :, None] * v_t[..., None, :]
                out = jnp.einsum('bhi,bhij->bhj', r_t, u * a + s)
                s = a + w_t[..., :, None] * s
                return (s, out)
            rkvw = tuple((jnp.moveaxis(t, 1, 0) for t in (r, k, v, w)))
            _, out = jax.lax.scan(step, s0, rkvw)
            out = jnp.moveaxis(out, 0, 1).reshape(b, l, e)
            og = out.reshape(b, l, h, s_)
            m = og.mean(-1, keepdims=True)
            va = ((og - m) ** 2).mean(-1, keepdims=True)
            og = ((og - m) / jnp.sqrt(va + 1e-05)).reshape(b, l, e) * gn_w + gn_b
            x1 = x + og * g @ Wo.T
            xc = _ln(x1, ln2_w, ln2_b)
            sx2 = jnp.concatenate([state[:, 0:1] - xc[:, :1], xc[:, :-1] - xc[:, 1:]], axis=1)
            xk2 = xc + sx2 * ffn_maa_k
            xr2 = xc + sx2 * ffn_maa_r
            rr = jax.nn.sigmoid(xr2 @ Wfr.T)
            kk = jnp.square(jax.nn.relu(xk2 @ Wfk.T))
            return x1 + rr * (kk @ Wfv.T)
        return _block(x, state, ln1_w, ln1_b, ln2_w, ln2_b, maa_x, maa_w1, maa_w2, maa_stack, time_decay, td_w1, td_w2, u, Wr, Wk, Wv, Wg, Wo, gn_w, gn_b, ffn_maa_k, ffn_maa_r, Wfk, Wfr, Wfv)

    def _L2_xattn_ref(x_this, x_other, Wg, bg, Wtheta, btheta, Wphi, bphi, Wz, bz, gamma, beta):
        import jax, jax.numpy as jnp
        import numpy as np
        B, C, CI, T = (8, 64, 32, 256)
        EPS = 1e-05
        g_x = jnp.einsum('oc,bct->bto', Wg, x_this) + bg
        theta = jnp.einsum('oc,bct->bot', Wtheta, x_this) + btheta[None, :, None]
        phi = jnp.einsum('oc,bct->bot', Wphi, x_other) + bphi[None, :, None]
        f = jnp.einsum('bci,bcj->bij', phi, theta)
        f_div_C = jax.nn.softmax(f, axis=-1)
        y = jnp.einsum('bij,bjo->bio', f_div_C, g_x)
        w_y = jnp.einsum('oc,btc->bot', Wz, y) + bz[None, :, None]
        mean = jnp.mean(w_y, axis=(0, 2), keepdims=True)
        var = jnp.var(w_y, axis=(0, 2), keepdims=True)
        w_y = gamma[None, :, None] * (w_y - mean) * jax.lax.rsqrt(var + EPS) + beta[None, :, None]
        return w_y + x_this

    def _L3_xattn_ref(hidden_states, audio_kv, audio_attention_mask, Wq, Wk, Wv, Wo, ln_gamma, ln_beta, gate):
        import jax, jax.numpy as jnp
        import numpy as np
        HIDDEN = 256
        HEADS = 16
        HEAD_DIM = HIDDEN // HEADS
        LN_EPS = 1e-05
        GATE_INIT = 0.5

        def _layer_norm(x, gamma, beta):
            mu = jnp.mean(x, axis=-1, keepdims=True)
            var = jnp.mean(jnp.square(x - mu), axis=-1, keepdims=True)
            return (x - mu) * jax.lax.rsqrt(var + LN_EPS) * gamma + beta
        B, Tt, D = hidden_states.shape
        Ta = audio_kv.shape[1]
        scale = HEAD_DIM ** (-0.5)
        a = _layer_norm(audio_kv, ln_gamma, ln_beta)
        Q = (hidden_states @ Wq.T).reshape(B, Tt, HEADS, HEAD_DIM).transpose(0, 2, 1, 3)
        K = (a @ Wk.T).reshape(B, Ta, HEADS, HEAD_DIM).transpose(0, 2, 1, 3)
        V = (a @ Wv.T).reshape(B, Ta, HEADS, HEAD_DIM).transpose(0, 2, 1, 3)
        scores = jnp.einsum('bhtd,bhsd->bhts', Q, K) * scale
        mask = audio_attention_mask[:, None, None, :]
        scores = jnp.where(mask, scores, jnp.float32(-jnp.inf))
        attn = jax.nn.softmax(scores, axis=-1)
        out = jnp.einsum('bhts,bhsd->bhtd', attn, V)
        out = out.transpose(0, 2, 1, 3).reshape(B, Tt, D)
        out = out @ Wo.T
        return hidden_states + jnp.tanh(gate) * out
    x = _L0_xattn_ref(x, ctx_2048, 0, L0_xattn_ln1_w, L0_xattn_ln1_b, L0_xattn_ln2_w, L0_xattn_ln2_b, L0_xattn_maa_x, L0_xattn_maa_w, L0_xattn_maa_k, L0_xattn_maa_v, L0_xattn_maa_r, L0_xattn_maa_g, L0_xattn_maa_w1, L0_xattn_maa_w2, L0_xattn_time_decay, L0_xattn_decay_w1, L0_xattn_decay_w2, L0_xattn_faaaa, L0_xattn_Wr, L0_xattn_Wk, L0_xattn_Wv, L0_xattn_Wg, L0_xattn_Wo, L0_xattn_gn_w, L0_xattn_gn_b, L0_xattn_fmaa_k, L0_xattn_fmaa_r, L0_xattn_fWk, L0_xattn_fWr, L0_xattn_fWv)
    x = _L1_xattn_ref(x, ctx_2048, L1_xattn_ln1_w, L1_xattn_ln1_b, L1_xattn_ln2_w, L1_xattn_ln2_b, L1_xattn_maa_x, L1_xattn_maa_w1, L1_xattn_maa_w2, L1_xattn_maa_stack, L1_xattn_time_decay, L1_xattn_td_w1, L1_xattn_td_w2, L1_xattn_u, L1_xattn_Wr, L1_xattn_Wk, L1_xattn_Wv, L1_xattn_Wg, L1_xattn_Wo, L1_xattn_gn_w, L1_xattn_gn_b, L1_xattn_ffn_maa_k, L1_xattn_ffn_maa_r, L1_xattn_Wfk, L1_xattn_Wfr, L1_xattn_Wfv)
    x = _L2_xattn_ref(x, ctx_2048, L2_xattn_Wg, L2_xattn_bg, L2_xattn_Wtheta, L2_xattn_btheta, L2_xattn_Wphi, L2_xattn_bphi, L2_xattn_Wz, L2_xattn_bz, L2_xattn_gamma, L2_xattn_beta)
    x = _L3_xattn_ref(x, ctx_2048, mask_BxS2_bf1, L3_xattn_Wq, L3_xattn_Wk, L3_xattn_Wv, L3_xattn_Wo, L3_xattn_ln_gamma, L3_xattn_ln_beta, L3_xattn_gate)
    return x

_drawn_inputs = setup_inputs


def setup_inputs(seed=0):
    import zlib

    import numpy as np

    out = dict(_drawn_inputs(seed))
    spreads = {'L0_xattn_ln1_w': (1.0, 0.6),
     'L0_xattn_ln1_b': (0.0, 0.654),
     'L0_xattn_ln2_w': (1.0, 0.6),
     'L0_xattn_ln2_b': (0.0, 0.8),
     'L0_xattn_gn_w': (1.0, 0.6),
     'L0_xattn_gn_b': (0.0, 0.8),
     'L1_xattn_ln1_w': (1.0, 0.6),
     'L1_xattn_ln1_b': (0.0, 2.0),
     'L1_xattn_ln2_w': (1.0, 0.6),
     'L1_xattn_ln2_b': (0.0, 2.0),
     'L1_xattn_gn_w': (1.0, 0.6),
     'L1_xattn_gn_b': (0.0, 2.0),
     'L2_xattn_bg': (0.0, 2.0),
     'L2_xattn_btheta': (0.0, 2.0),
     'L2_xattn_bphi': (0.0, 2.0),
     'L2_xattn_bz': (0.0, 2.0),
     'L3_xattn_ln_gamma': (1.0, 0.6),
     'L3_xattn_ln_beta': (0.0, 2.0)}
    factors = {'L0_xattn_maa_x': 8.0,
     'L0_xattn_maa_w': 8.0,
     'L0_xattn_maa_v': 2.823,
     'L0_xattn_maa_g': 2.814,
     'L0_xattn_maa_w1': 8.0,
     'L0_xattn_maa_w2': 8.0,
     'L0_xattn_time_decay': 4.169,
     'L0_xattn_decay_w1': 8.0,
     'L0_xattn_decay_w2': 8.0,
     'L0_xattn_faaaa': 8.0,
     'L0_xattn_fmaa_k': 8.0,
     'L0_xattn_fmaa_r': 8.0,
     'L0_xattn_fWk': 5.139,
     'L0_xattn_fWr': 8.0,
     'L0_xattn_fWv': 4.673,
     'L1_xattn_maa_x': 64.0,
     'L1_xattn_maa_w1': 64.0,
     'L1_xattn_maa_w2': 64.0,
     'L1_xattn_maa_stack': 26.104,
     'L1_xattn_time_decay': 28.232,
     'L1_xattn_td_w1': 64.0,
     'L1_xattn_td_w2': 64.0,
     'L1_xattn_u': 54.0,
     'L1_xattn_ffn_maa_k': 33.358,
     'L1_xattn_ffn_maa_r': 47.699,
     'L1_xattn_Wfk': 10.263,
     'L1_xattn_Wfr': 36.538,
     'L1_xattn_Wfv': 8.932,
     'L3_xattn_Wq': 64.0,
     'L3_xattn_Wk': 64.0,
     'L3_xattn_Wv': 29.432,
     'L3_xattn_Wo': 29.736,
     'L1_xattn_Wr': 8.0,
     'L1_xattn_Wk': 8.0,
     'L1_xattn_Wv': 8.0,
     'L1_xattn_Wg': 8.0,
     'L1_xattn_Wo': 8.0,
     'L2_xattn_Wg': 55.803,
     'L2_xattn_Wtheta': 56.514,
     'L2_xattn_Wphi': 60.563,
     'L2_xattn_Wz': 57.38,
     'L2_xattn_gamma': 54.31,
     'L2_xattn_beta': 57.538}
    for name, (base, spread) in spreads.items():
        noise = np.random.default_rng([zlib.crc32(name.encode()), seed]).standard_normal(out[name].shape)
        drawn = base * np.exp(spread * noise) if base else spread * noise
        out[name] = jnp.asarray(drawn.astype(out[name].dtype))
    for name, factor in factors.items():
        out[name] = (out[name] * factor).astype(out[name].dtype)
    return out
```

```python
from contextlib import ExitStack

import concourse.bass as bass
from concourse import mybir
from concourse.alu_op_type import AluOpType as ALU

F32 = mybir.dt.float32
F32R = mybir.dt.float32r
U8 = mybir.dt.uint8
ACT = mybir.ActivationFunctionType
AX = mybir.AxisListType.X

P = 128
B, L, C, S = 32, 64, 256, 8
HALF = C // P
NT = B * L // P
GB = 8
GT = GB * L // P
N = GB * L
G = B // GB
ITEMS = 2 * G
DM, DD = 32, 64
F = 5
EPS = 1e-5
UNITS = S * HALF
RING = 4
LAG = 2

P_W1, P_D1, P_PROJ = 0, HALF * F * DM, HALF * (F * DM + DD)
P_W2A = P_PROJ + 4 * HALF * C
P_W2B, P_D2, P_VEC = P_W2A + C, P_W2A + 2 * C, P_W2A + 3 * C
V_LNW, V_LNB, V_MAAX, V_MAAF, V_TD, V_U = 0, 2, 4, 6, 16, 18
P_COLS = P_VEC + 20
F_WO, F_K, F_R, F_V, F_VEC = (i * HALF * C for i in range(5))
V_LN2W, V_LN2B, V_GNW, V_GNB, V_FK, V_FR = range(0, 12, 2)
F_COLS = F_VEC + 12
C_RED, C_CEN, C_ONE, C_ID, C_AVG = 0, S * P, (S + 1) * P, (S + 2) * P, (S + 3) * P
C_COLS = C_AVG + P // S


def first(n):
    return isinstance(n, int) and n == 0


def sweep2(eng, body, count):
    body(0, 0, 1, None, 2)
    with eng.Fori(0, (count - 4) // 2) as i:
        body(2 * i + 1, 1, 2 * i + 2, 2 * i, 2 * i + 3)
        body(2 * i + 2, 0, 2 * i + 3, 2 * i + 1, 2 * i + 4)
    body(count - 3, 1, count - 2, count - 4, count - 1)
    body(count - 2, 0, count - 1, count - 3, None)
    body(count - 1, 1, None, count - 2, None)


def rwkv_phase(nc, ctx, A, xres, sb, sem, psum):
    cst = sb("cst", [P, C_COLS])
    rep_r = sb("rep_r", [P, S * P], F32R)
    wp = sb("wp", [P, P_COLS])
    wf = sb("wf", [P, F_COLS])
    s0 = sb("s0", [P, HALF, S, B])
    shift = sb("shift", [P, 2, HALF, B])
    eps = sb("eps", [P, 1])
    fence = sb("fence", [P, 1])
    neg_half = sb("neg_half", [P, GT])
    xn = sb("xn", [P, GT, C])
    st6 = sb("st6", [P, GT, 6])
    mv = sb("mv", [P, GT, 2])
    ve = sb("ve", [P, GT])
    rstd = sb("rstd", [P, GT])
    xa = sb("xa", [P, HALF, GB, L + 1])
    sx = sb("sx", [P, HALF, GB, L])
    xxx = sb("xxx", [P, HALF, N])
    tt = sb("tt", [P, N])
    tg = sb("tg", [DM, N])
    xf = sb("xf", [P, F, HALF, GB, L])
    td = sb("td", [DD, N])
    ew = sb("ew", [P, HALF, GB, L])
    vx = sb("vx", [P, HALF, GB, L + 1])
    gth = xxx[:]
    ruk = ew[:].rearrange("p h b l -> p h (b l)")
    kx = sb("kx", [P, 2, HALF, GB, L + 1])
    wx = sb("wx", [P, 2, HALF, GB, L])
    vhi = sb("vhi", [P, 2, HALF, GB, L], F32R)
    vlo = sb("vlo", [P, 2, HALF, GB, L], F32R)
    rr = sb("rr", [P, 2, HALF, N])
    av = sb("av", [P, 2, HALF, N])
    g2 = sb("g2", [P, 2, HALF, N])
    st = sb("st", [P, RING, N])
    rs = sb("rs", [P, RING, N])
    yc = sb("yc", [P, HALF, N])
    sq = sb("sq", [P, HALF, N])
    gsd = sb("gsd", [P, GT * HALF * 16])
    grs = sb("grs", [P, GT * HALF * 16])
    grx = sb("grx", [P, GT, HALF, 16, S])
    z = sb("z", [P, HALF, N])
    yg = sb("yg", [P, HALF, N])
    xn2 = yc[:].rearrange("p h (t c) -> p (h t) c", c=C)
    st62 = sb("st62", [P, GT, 6])
    mv2 = sb("mv2", [P, GT, 2])
    ve2 = sb("ve2", [P, GT])
    rstd2 = sb("rstd2", [P, GT])
    xc = sb("xc", [P, HALF, GB, L + 1])
    sxc = sb("sxc", [P, HALF, GB, L])
    xk2 = yg[:].rearrange("p h (b l) -> p h b l", b=GB)
    xr2 = sb("xr2", [P, HALF, GB, L])
    kr = z[:]
    fth = sq[:]
    ft = sxc[:].rearrange("p h b l -> p h (b l)")

    PA, PY, PP, PF = psum[0:2], psum[2:4], psum[4:6], psum[6:8]

    names = ("x_in consts_in pw_in fw_in rep_cast inits pads "
             "ln1_stats ln1_ve ln1_rstd x_norm x_tr xa_half xa_first sx_ready xxx_half w1_prod t_tanh mix_prod "
             "mix_scaled xf_ready d1_prod d_tanh d2_prod decay_exp decay k_prod k_ready v_prod v_ready vhi_ready "
             "vlo_ready r_prod r_ready g_prod g_tanh g_ready ruk_ready bonus_prod bonus "
             "v_spread kv_prod state rs_prod reduced "
             "y_copied y_squared gn_var gn_sd gn_rstd gn_spread gn_tr y_scaled y_affine y_gated wo_prod x_mid "
             "ln2_stats ln2_ve ln2_rstd x_norm2 x_tr2 xc_half xc_first sxc_ready xk2_half xr2_half fk_prod "
             "fk_relu fk_square fr_prod fr_tanh fv_prod fv_gated x_out").split()
    s = type("Sems", (), {n: sem(n) for n in names})

    def lw(off, kh, m0, m, cols):
        return wp[:, off + kh * cols + m0:off + kh * cols + m0 + m]

    def proj(i, kh, half):
        return lw(P_PROJ + i * HALF * C, kh, half * P, P, C)

    def vec(w, base, v, i):
        return w[:, base + v + i:base + v + i + 1]

    def cc(off, n=P):
        return cst[:, off:off + n]

    def flat(ap):
        return ap.rearrange("p b l -> p (b l)")

    block = ctx.enter_context(nc.Block())

    @block.sync
    def _(sp):
        sp.dma_start(xres[:], A["x"]).then_inc(s.x_in, 16)
        sp.dma_start(wp[:], A["wp"][0]).then_inc(s.pw_in, 16)
        for dst, src in ((xf[:, 0].rearrange("p h b l -> p (h b l)"), A["rep"]), (cst[:], A["cst"]), (s0[:], A["s0"]), (shift[:], A["shift"])):
            sp.dma_start(dst, src).then_inc(s.consts_in, 16)
        sp.dma_start(wf[:], A["wf"][0]).then_inc(s.fw_in, 16)
        sp.wait_ge(s.bonus, HALF * G)
        sp.dma_start(wp[:], A["wp"][1]).then_inc(s.pw_in, 16)
        sp.wait_ge(s.x_out, 2 * G)
        sp.dma_start(wf[:], A["wf"][1]).then_inc(s.fw_in, 16)

    def layer(n):
        return n // G

    def tile0(n):
        return (n % G) * GT

    @block.tensor
    def _(pe):
        ident = cc(C_ID)

        def x_transposes(m, src, norm_sem, bank, done):
            pe.wait_ge(norm_sem, GT * (m + 1))
            for half in range(HALF):
                for t in range(GT):
                    last = pe.transpose(bank[half][:, t * P:(t + 1) * P], src[:, t, half * P:(half + 1) * P], ident)
                last.then_inc(done, 1)

        def p_tr(m):
            if not first(m):
                pe.wait_ge(s.bonus, HALF * m)
            x_transposes(m, xn, s.x_norm, PP, s.x_tr)

        def p_w1(m):
            pe.wait_ge(s.pw_in, 16 * (layer(m) + 1))
            pe.wait_ge(s.xxx_half, HALF * (m + 1))
            pe.wait_ge(s.xa_half, HALF * (m + 1))
            for kh in range(HALF):
                a = pe.matmul(PP[0][:], lw(P_W1, kh, 0, P, F * DM), xxx[:, kh, :], start=kh == 0, stop=kh == HALF - 1)
            a.then_inc(s.w1_prod, 1)
            for kh in range(HALF):
                a = pe.matmul(PP[1][0:DM, :], lw(P_W1, kh, P, DM, F * DM), xxx[:, kh, :],
                              start=kh == 0, stop=kh == HALF - 1)
            a.then_inc(s.w1_prod, 1)

        def p_mix(m, f):
            for half in range(HALF):
                if f == 0:
                    pe.wait_ge(s.t_tanh, 2 * (m + 1))
                else:
                    pe.wait_ge(s.mix_scaled, F * HALF * m + (f - 1) * HALF + half + 1)
                if f < 4:
                    w, t = wp[f * DM:(f + 1) * DM, P_W2A + half * P:P_W2A + (half + 1) * P], tt[f * DM:(f + 1) * DM, :]
                else:
                    w, t = wp[0:DM, P_W2B + half * P:P_W2B + (half + 1) * P], tg[:, :]
                pe.matmul(PP[half][:], w, t, start=True, stop=True).then_inc(s.mix_prod, 1)

        def xin(f, kh):
            return flat(xf[:, f, kh])

        def p_d1(m):
            pe.wait_ge(s.mix_scaled, F * HALF * m + F * HALF)
            pe.wait_ge(s.xf_ready, F * HALF * m + HALF)
            for kh in range(HALF):
                a = pe.matmul(PP[0][0:DD, :], lw(P_D1, kh, 0, DD, DD), xin(0, kh), start=kh == 0, stop=kh == HALF - 1)
            a.then_inc(s.d1_prod, 1)

        def p_d2(m):
            pe.wait_ge(s.d_tanh, m + 1)
            for half in range(HALF):
                pe.matmul(PP[half][:], wp[0:DD, P_D2 + half * P:P_D2 + (half + 1) * P], td[:],
                          start=True, stop=True).then_inc(s.d2_prod, 1)

        def p_proj(m, i, freed, done):
            pe.wait_ge(s.xf_ready, F * HALF * m + (i + 2) * HALF)
            for half in range(HALF):
                pe.wait_ge(freed, HALF * m + half + 1)
                for kh in range(HALF):
                    a = pe.matmul(PP[half][:], proj(i, kh, half), xin(i + 1, kh), start=kh == 0, stop=kh == HALF - 1)
                a.then_inc(done, 1)

        def p_bonus(m):
            for half in range(HALF):
                pe.wait_ge(s.ruk_ready, HALF * m + half + 1)
                pe.wait_ge(s.g_ready, HALF * m + half + 1)
                pe.matmul(PP[half][:], cc(C_ONE), ruk[:, half], start=True, stop=True).then_inc(s.bonus_prod, 1)

        def w_spread(n, par, q):
            j, half = q // HALF, q % HALF
            if not (first(n) and q < 2):
                pe.wait_ge(s.state, UNITS * n + q - 1)
            rep = rep_r[:, j * P:(j + 1) * P]
            pe.matmul(PA[half][:], rep, flat(vhi[:, par, half]), start=True, stop=False)
            pe.matmul(PA[half][:, 0:N:L], ident, s0[:, half, j, bass.ds((n % G) * GB, GB)],
                      start=False, stop=True, skip_group_check=True)
            pe.matmul(PA[half][:], rep, flat(vlo[:, par, half]), start=False,
                      stop=True).then_inc(s.v_spread, 1)

        def w_reduce(n, q):
            j, half = q // HALF, q % HALF
            pe.wait_ge(s.rs_prod, UNITS * n + q + 1)
            pe.matmul(PY[half][:], cc(C_RED + j * P), rs[:, q % RING], start=False,
                      stop=j == S - 1).then_inc(s.reduced, 1)

        def w_bonus(n, par):
            pe.wait_ge(s.bonus, HALF * (n + 1))
            if not first(n):
                pe.wait_ge(s.y_copied, HALF * n)
            for half in range(HALF):
                pe.matmul(PY[half][:], cc(C_CEN), av[:, par, half], start=True, stop=False)

        def f_var(m):
            pe.wait_ge(s.y_squared, HALF * (m + 1))
            for t in range(GT):
                for half in range(HALF):
                    o = (t * HALF + half) * 16
                    a = pe.matmul(PF[0][:, o:o + 16], sq[:, half, t * P:(t + 1) * P], cc(C_AVG, 16),
                                  start=True, stop=True)
            a.then_inc(s.gn_var, 1)

        def f_gtr(m):
            pe.wait_ge(s.gn_spread, m + 1)
            for half in range(HALF):
                for t in range(GT):
                    a = pe.transpose(PF[half][:, t * P:(t + 1) * P], grx[:, t, half].rearrange("p h j -> p (h j)"),
                                     ident)
                a.then_inc(s.gn_tr, 1)

        def token_product(m, src, off, waits, done):
            for pair in range(2):
                for sm, c in waits(pair):
                    pe.wait_ge(sm, c)
                for t in range(2):
                    tile = 2 * pair + t
                    for kh in range(HALF):
                        a = pe.matmul(PF[pair][:, t * C:(t + 1) * C], src(kh)[:, tile * P:(tile + 1) * P],
                                      wf[:, off + kh * C:off + (kh + 1) * C], start=kh == 0, stop=kh == HALF - 1)
                a.then_inc(done, 1)

        def f_wo(m):
            pe.wait_ge(s.fw_in, 16 * (layer(m) + 1))
            token_product(m, lambda kh: yg[:, kh], F_WO, lambda pair: [(s.y_gated, HALF * (m + 1))], s.wo_prod)

        def f_tr(m):
            pe.wait_ge(s.x_mid, 2 * (m + 1))
            x_transposes(m, xn2, s.x_norm2, PF, s.x_tr2)

        def f_k(m):
            pe.wait_ge(s.xk2_half, HALF * (m + 1))
            for half in range(HALF):
                pe.wait_ge(s.xc_half, HALF * m + half + 1)
                for kh in range(HALF):
                    o = F_K + kh * C + half * P
                    a = pe.matmul(PF[half][:], wf[:, o:o + P], flat(xk2[:, kh]), start=kh == 0, stop=kh == HALF - 1)
                a.then_inc(s.fk_prod, 1)

        def f_r(m):
            pe.wait_ge(s.xr2_half, HALF * (m + 1))
            token_product(m, lambda kh: flat(xr2[:, kh]), F_R, lambda pair: [(s.fk_relu, HALF * m + pair + 1)],
                          s.fr_prod)

        def f_v(m):
            pe.wait_ge(s.fk_square, HALF * (m + 1))
            token_product(m, lambda kh: kr[:, kh], F_V, lambda pair: [(s.fr_tanh, 2 * m + pair + 1)], s.fv_prod)

        def projections(m, i):
            p_proj(m, i, *[(s.decay_exp, s.k_prod), (s.k_ready, s.v_prod), (s.vlo_ready, s.r_prod),
                           (s.r_ready, s.g_prod)][i])

        def body(n, par, p, f, p2):
            pe.wait_ge(s.vlo_ready, HALF * (n + 1))
            w_spread(n, par, 0)
            for q in range(UNITS):
                if q + 1 < UNITS:
                    w_spread(n, par, q + 1)
                if q < LAG:
                    if f is not None:
                        w_reduce(f, q + UNITS - LAG)
                elif q > LAG:
                    w_reduce(n, q - LAG)
                if p is not None:
                    if q == 0:
                        p_w1(p)
                    if 1 <= q < 6:
                        p_mix(p, q - 1)
                    if q == 6:
                        p_d1(p)
                    if q == 7:
                        p_d2(p)
                    if 8 <= q < 12:
                        projections(p, q - 8)
                    if q == 12:
                        p_bonus(p)
                if p2 is not None and q == 14:
                    p_tr(p2)
                if f is not None:
                    if q == 2:
                        f_var(f)
                    if q == 3:
                        f_gtr(f)
                    if q == 5:
                        f_wo(f)
                    if q == 8:
                        f_tr(f)
                    if q == 11:
                        f_k(f)
                    if q == 13:
                        f_r(f)
                    if q == 15:
                        f_v(f)
                if q == LAG:
                    w_bonus(n, par)
                    w_reduce(n, 0)

        pe.wait_ge(s.consts_in, 64)
        pe.wait_ge(s.rep_cast, 1)
        pe.wait_ge(s.pads, 2)
        p_tr(0)
        p_w1(0)
        for f in range(F):
            p_mix(0, f)
        p_d1(0)
        p_d2(0)
        for i in range(4):
            projections(0, i)
        p_bonus(0)
        p_tr(1)
        sweep2(pe, body, ITEMS)
        last = ITEMS - 1
        for q in range(UNITS - LAG, UNITS):
            w_reduce(last, q)
        f_var(last)
        f_gtr(last)
        f_wo(last)
        f_tr(last)
        f_k(last)
        f_r(last)
        f_v(last)

    @block.vector
    def _(v):
        def layer_norm(m, st6, mv, ve, rstd, xn, stats, ve_sem, rstd_sem, done):
            v.memset(fence[:], 0.0)
            for t in range(GT):
                v.bn_stats(st6[:, t], xres[:, bass.ds(tile0(m) + t, 1), :].rearrange("p t c -> p (t c)")).then_inc(stats, 1)
            v.wait_ge(stats, 2 * GT * m + GT)
            v.memset(fence[:], 0.0)
            for t in range(GT):
                v.bn_aggr(mv[:, t], st6[:, t]).then_inc(stats, 1)
            v.wait_ge(stats, 2 * GT * (m + 1))
            v.tensor_scalar(ve[:], mv[:, :, 1], EPS, None, ALU.add).then_inc(ve_sem, 1)
            v.wait_ge(rstd_sem, m + 1)
            for t in range(GT):
                v.tensor_scalar(xn[:, t], xres[:, bass.ds(tile0(m) + t, 1), :].rearrange("p t c -> p (t c)"),
                                mv[:, t, 0:1], rstd[:, t:t + 1], ALU.subtract, ALU.mult).then_inc(done, 1)

        def p_ln(m):
            layer_norm(m, st6, mv, ve, rstd, xn, s.ln1_stats, s.ln1_ve, s.ln1_rstd, s.x_norm)

        def p_shift(m):
            v.wait_ge(s.xa_half, HALF * (m + 1))
            v.wait_ge(s.xa_first, m + 1)
            v.tensor_tensor(sx[:].rearrange("p h b l -> p (h b) l"), xa[:, :, :, 0:L].rearrange("p h b l -> p (h b) l"),
                            xa[:, :, :, 1:L + 1].rearrange("p h b l -> p (h b) l"), ALU.subtract).then_inc(s.sx_ready, 1)
            v.wait_ge(s.sx_ready, m + 1)
            for half in range(HALF):
                v.scalar_tensor_tensor(out=xxx[:, half].rearrange("p (b l) -> p b l", b=GB), in0=sx[:, half],
                                       scalar=vec(wp, P_VEC, V_MAAX, half), in1=xa[:, half, :, 1:L + 1],
                                       op0=ALU.mult, op1=ALU.add).then_inc(s.xxx_half, 1)

        def p_mix(m, f):
            for half in range(HALF):
                v.wait_ge(s.mix_prod, F * HALF * m + f * HALF + half + 1)
                v.scalar_tensor_tensor(out=flat(xf[:, f, half]), in0=PP[half][:],
                                       scalar=vec(wp, P_VEC, V_MAAF + f * HALF, half), in1=flat(sx[:, half]),
                                       op0=ALU.add, op1=ALU.mult).then_inc(s.mix_scaled, 1)

        def shifted(bank):
            return bank[:].rearrange("p (b l) -> p b l", b=GB)[:, :, 0:L - 1]

        def p_vlo(m, par):
            for half in range(HALF):
                v.wait_ge(s.vhi_ready, HALF * m + half + 1)
                v.tensor_tensor(vlo[:, par, half, :, 1:L], shifted(PP[half]),
                                vhi[:, par, half, :, 1:L].bitcast(F32), ALU.subtract).then_inc(s.vlo_ready, 1)

        def p_gate(m, par):
            for half in range(HALF):
                v.wait_ge(s.g_tanh, HALF * m + half + 1)
                v.scalar_tensor_tensor(out=g2[:, par, half], in0=gth[:, half], scalar=1.0, in1=PP[half][:],
                                       op0=ALU.add, op1=ALU.mult).then_inc(s.g_ready, 1)

        def p_ruk(m, par):
            v.wait_ge(s.r_ready, HALF * (m + 1))
            for half in range(HALF):
                v.scalar_tensor_tensor(out=ruk[:, half].rearrange("p (b l) -> p b l", b=GB),
                                       in0=rr[:, par, half].rearrange("p (b l) -> p b l", b=GB),
                                       scalar=vec(wp, P_VEC, V_U, half), in1=kx[:, par, half, :, 1:L + 1],
                                       op0=ALU.mult, op1=ALU.mult).then_inc(s.ruk_ready, 1)

        def p_av(m, par):
            for half in range(HALF):
                v.wait_ge(s.bonus_prod, HALF * m + half + 1)
                v.tensor_tensor(av[:, par, half].rearrange("p (b l) -> p b l", b=GB),
                                PP[half][:].rearrange("p (b l) -> p b l", b=GB), vx[:, half, :, 1:L + 1],
                                ALU.mult).then_inc(s.bonus, 1)

        def w_kv(n, par, q):
            half = q % HALF
            v.wait_ge(s.v_spread, UNITS * n + q + 1)
            bank = PA[half][:].rearrange("p (b l) -> p b l", b=GB)
            v.tensor_tensor(bank, kx[:, par, half, :, 0:L], bank, ALU.mult).then_inc(s.kv_prod, 1)

        def w_scan(n, par, q):
            half = q % HALF
            v.wait_ge(s.kv_prod, UNITS * n + q + 1)
            if not (first(n) and q < RING):
                v.wait_ge(s.rs_prod, UNITS * n + q - RING + 1)
            v.tensor_tensor_scan(st[:, q % RING], flat(wx[:, par, half]), PA[half][:], 0.0,
                                 ALU.mult, ALU.add).then_inc(s.state, 1)

        def f_rstd(m):
            v.wait_ge(s.gn_sd, m + 1)
            v.reciprocal(grs[:], gsd[:]).then_inc(s.gn_rstd, 1)
            v.wait_ge(s.gn_rstd, m + 1)
            v.tensor_copy(grx[:].rearrange("p t f h j -> p (t f h) j"),
                          grs[:].unsqueeze(2).broadcast_to([P, GT * HALF * 16, S])).then_inc(s.gn_spread, 1)

        def f_scale(m):
            for half in range(HALF):
                v.wait_ge(s.gn_tr, HALF * m + half + 1)
                v.tensor_tensor(z[:, half], yc[:, half], PF[half][:], ALU.mult).then_inc(s.y_scaled, 1)

        def f_gate(m, par):
            for half in range(HALF):
                v.wait_ge(s.y_affine, HALF * m + half + 1)
                v.scalar_tensor_tensor(out=yg[:, half], in0=z[:, half], scalar=0.5, in1=g2[:, par, half],
                                       op0=ALU.mult, op1=ALU.mult).then_inc(s.y_gated, 1)

        def tiles(m, pair):
            return xres[:, bass.ds(tile0(m) + 2 * pair, 2), :].rearrange("p t c -> p (t c)")

        def f_mid(m):
            for pair in range(2):
                v.wait_ge(s.wo_prod, 2 * m + pair + 1)
                v.tensor_tensor(tiles(m, pair), tiles(m, pair), PF[pair][:], ALU.add).then_inc(s.x_mid, 1)
            v.wait_ge(s.x_mid, 2 * (m + 1))

        def f_ln(m):
            layer_norm(m, st62, mv2, ve2, rstd2, xn2, s.ln2_stats, s.ln2_ve, s.ln2_rstd, s.x_norm2)

        def f_shift(m):
            v.wait_ge(s.xc_half, HALF * (m + 1))
            v.wait_ge(s.xc_first, m + 1)
            v.tensor_tensor(sxc[:].rearrange("p h b l -> p (h b) l"), xc[:, :, :, 0:L].rearrange("p h b l -> p (h b) l"),
                            xc[:, :, :, 1:L + 1].rearrange("p h b l -> p (h b) l"), ALU.subtract).then_inc(s.sxc_ready, 1)
            v.wait_ge(s.sxc_ready, m + 1)
            for out, vi, done in ((xk2, V_FK, s.xk2_half), (xr2, V_FR, s.xr2_half)):
                for half in range(HALF):
                    v.scalar_tensor_tensor(out=out[:, half], in0=sxc[:, half], scalar=vec(wf, F_VEC, vi, half),
                                           in1=xc[:, half, :, 1:L + 1], op0=ALU.mult, op1=ALU.add).then_inc(done, 1)

        def f_out(m):
            for pair in range(2):
                v.wait_ge(s.fv_prod, 2 * m + pair + 1)
                v.scalar_tensor_tensor(out=ft[:, pair], in0=fth[:, pair], scalar=1.0, in1=PF[pair][:],
                                       op0=ALU.add, op1=ALU.mult).then_inc(s.fv_gated, 1)
                v.wait_ge(s.fv_gated, 2 * m + pair + 1)
                v.scalar_tensor_tensor(out=tiles(m, pair), in0=ft[:, pair], scalar=0.5, in1=tiles(m, pair),
                                       op0=ALU.mult, op1=ALU.add).then_inc(s.x_out, 1)
            v.wait_ge(s.x_out, 2 * (m + 1))

        def body(n, par, p, f, p2):
            for q in range(UNITS):
                w_kv(n, par, q)
                w_scan(n, par, q)
                if p is not None:
                    if 1 <= q < 6:
                        p_mix(p, q - 1)
                    if q == 9:
                        p_vlo(p, 1 - par)
                    if q == 11:
                        p_ruk(p, 1 - par)
                        p_gate(p, 1 - par)
                    if q == 12:
                        p_av(p, 1 - par)
                if p2 is not None:
                    if q == 13:
                        p_ln(p2)
                    if q == 15:
                        p_shift(p2)
                if f is not None:
                    if q == 2:
                        f_rstd(f)
                    if q == 3:
                        f_scale(f)
                    if q == 4:
                        f_gate(f, 1 - par)
                    if q == 5:
                        f_mid(f)
                    if q == 6:
                        f_ln(f)
                    if q == 8:
                        f_shift(f)
                    if q == 15:
                        f_out(f)

        v.memset(eps[:], EPS).then_inc(s.inits, 1)
        v.memset(neg_half[:], -0.5).then_inc(s.inits, 1)
        v.memset(kx[:, :, :, :, 0:1].rearrange("p a h b l -> p (a h b) l"), 1.0).then_inc(s.inits, 1)
        v.memset(wx[:, :, :, :, 0:1].rearrange("p a h b l -> p (a h b) l"), 0.0).then_inc(s.inits, 1)
        v.memset(vx[:, :, :, 0:1].rearrange("p h b l -> p (h b) l"), 0.0).then_inc(s.inits, 1)
        v.wait_ge(s.consts_in, 64)
        v.tensor_copy(rep_r[:], xf[:, 0].rearrange("p h b l -> p (h b l)")).then_inc(s.rep_cast, 1)
        v.wait_ge(s.inits, 5)
        for t in (vhi, vlo):
            v.tensor_copy(t[:, :, :, :, 0:1].rearrange("p a h b l -> p (a h b) l"),
                          wx[:, :, :, :, 0:1].rearrange("p a h b l -> p (a h b) l")).then_inc(s.pads, 1)
        v.wait_ge(s.x_in, 16)
        v.wait_ge(s.pw_in, 16)
        p_ln(0)
        p_shift(0)
        for f in range(F):
            p_mix(0, f)
        p_vlo(0, 0)
        p_ruk(0, 0)
        p_gate(0, 0)
        p_av(0, 0)
        p_ln(1)
        p_shift(1)
        sweep2(v, body, ITEMS)
        last = ITEMS - 1
        f_rstd(last)
        f_scale(last)
        f_gate(last, 1)
        f_mid(last)
        f_ln(last)
        f_shift(last)
        f_out(last)

    @block.scalar
    def _(act):
        def bl(ap):
            return ap.rearrange("p (b l) -> p b l", b=GB)

        def p_xa(m):
            act.wait_ge(s.pw_in, 16 * (layer(m) + 1))
            for half in range(HALF):
                act.wait_ge(s.x_tr, HALF * m + half + 1)
                act.activation(xa[:, half, :, 1:L + 1], bl(PP[half][:]), ACT.Identity,
                               bias=vec(wp, P_VEC, V_LNB, half), scale=vec(wp, P_VEC, V_LNW, half)).then_inc(s.xa_half, 1)

        def p_tanh(m):
            act.wait_ge(s.w1_prod, 2 * m + 1)
            act.activation(tt[:], PP[0][:], ACT.Tanh).then_inc(s.t_tanh, 1)
            act.wait_ge(s.w1_prod, 2 * m + 2)
            act.activation(tg[:], PP[1][0:DM, :], ACT.Tanh).then_inc(s.t_tanh, 1)

        def p_dtanh(m):
            act.wait_ge(s.d1_prod, m + 1)
            act.activation(td[:], PP[0][0:DD, :], ACT.Tanh).then_inc(s.d_tanh, 1)

        def p_decay(m, par):
            for half in range(HALF):
                act.wait_ge(s.d2_prod, HALF * m + half + 1)
                act.activation(flat(ew[:, half]), PP[half][:], ACT.Exp, bias=vec(wp, P_VEC, V_TD, half)).then_inc(s.decay_exp, 1)
            act.wait_ge(s.decay_exp, HALF * (m + 1))
            for half in range(HALF):
                act.activation(wx[:, par, half, :, 1:L], ew[:, half, :, 0:L - 1], ACT.Exp, scale=-1.0).then_inc(s.decay, 1)

        def p_k(m, par):
            for half in range(HALF):
                act.wait_ge(s.k_prod, HALF * m + half + 1)
                act.copy(kx[:, par, half, :, 1:L + 1], bl(PP[half][:])).then_inc(s.k_ready, 1)

        def p_v(m, par):
            for half in range(HALF):
                act.wait_ge(s.v_prod, HALF * m + half + 1)
                act.copy(vx[:, half, :, 1:L + 1], bl(PP[half][:])).then_inc(s.v_ready, 1)
                act.copy(vhi[:, par, half, :, 1:L], bl(PP[half][:])[:, :, 0:L - 1]).then_inc(s.vhi_ready, 1)

        def p_r(m, par):
            for half in range(HALF):
                act.wait_ge(s.r_prod, HALF * m + half + 1)
                act.copy(rr[:, par, half], PP[half][:]).then_inc(s.r_ready, 1)

        def p_g(m):
            for half in range(HALF):
                act.wait_ge(s.g_prod, HALF * m + half + 1)
                act.activation(gth[:, half], PP[half][:], ACT.Tanh, scale=0.5).then_inc(s.g_tanh, 1)

        def f_y(m):
            act.wait_ge(s.reduced, UNITS * (m + 1))
            for half in range(HALF):
                act.activation(sq[:, half], PY[half][:], ACT.Square).then_inc(s.y_squared, 1)
                act.copy(yc[:, half], PY[half][:]).then_inc(s.y_copied, 1)

        def f_sd(m):
            act.wait_ge(s.gn_var, m + 1)
            act.activation(gsd[:], PF[0][:, 0:GT * HALF * 16], ACT.Sqrt, bias=eps[:, 0:1]).then_inc(s.gn_sd, 1)

        def f_affine(m):
            for half in range(HALF):
                act.wait_ge(s.y_scaled, HALF * m + half + 1)
                act.activation(z[:, half], z[:, half], ACT.Identity, bias=vec(wf, F_VEC, V_GNB, half),
                               scale=vec(wf, F_VEC, V_GNW, half)).then_inc(s.y_affine, 1)

        def f_xc(m):
            for half in range(HALF):
                act.wait_ge(s.x_tr2, HALF * m + half + 1)
                act.activation(xc[:, half, :, 1:L + 1], bl(PF[half][:]), ACT.Identity,
                               bias=vec(wf, F_VEC, V_LN2B, half), scale=vec(wf, F_VEC, V_LN2W, half)).then_inc(s.xc_half, 1)

        def f_k(m):
            for half in range(HALF):
                act.wait_ge(s.fk_prod, HALF * m + half + 1)
                act.activation(kr[:, half], PF[half][:], ACT.Relu).then_inc(s.fk_relu, 1)
                act.wait_ge(s.fk_relu, HALF * m + half + 1)
                act.activation(kr[:, half], kr[:, half], ACT.Square).then_inc(s.fk_square, 1)

        def f_r(m):
            for pair in range(2):
                act.wait_ge(s.fr_prod, 2 * m + pair + 1)
                act.activation(fth[:, pair], PF[pair][:], ACT.Tanh, scale=0.5).then_inc(s.fr_tanh, 1)

        def body(n, par, p, f, p2):
            for q in range(UNITS):
                if p is not None:
                    if q == 0:
                        p_tanh(p)
                    if q == 6:
                        p_dtanh(p)
                    if q == 7:
                        p_decay(p, 1 - par)
                    if q == 8:
                        p_k(p, 1 - par)
                    if q == 9:
                        p_v(p, 1 - par)
                    if q == 10:
                        p_r(p, 1 - par)
                    if q == 11:
                        p_g(p)
                if p2 is not None and q == 14:
                    p_xa(p2)
                if f is not None:
                    if q == 1:
                        act.wait_ge(s.fw_in, 16 * (layer(f) + 1))
                        f_y(f)
                        f_sd(f)
                    if q == 3:
                        f_affine(f)
                    if q == 8:
                        f_xc(f)
                    if q == 11:
                        f_k(f)
                    if q == 13:
                        f_r(f)

        act.wait_ge(s.inits, 5)
        p_xa(0)
        p_tanh(0)
        p_dtanh(0)
        p_decay(0, 0)
        p_k(0, 0)
        p_v(0, 0)
        p_r(0, 0)
        p_g(0)
        p_xa(1)
        sweep2(act, body, ITEMS)
        last = ITEMS - 1
        act.wait_ge(s.x_out, 2 * last)
        f_y(last)
        f_sd(last)
        f_affine(last)
        f_xc(last)
        f_k(last)
        f_r(last)

    @block.gpsimd
    def _(gp):
        def p_first(m):
            if not first(m):
                gp.wait_ge(s.xf_ready, F * HALF * m)
            gp.tensor_copy(xa[:, :, :, 0:1].rearrange("p h b l -> p h (b l)"),
                           shift[:, 0, :, bass.ds((m % G) * GB, GB)]).then_inc(s.xa_first, 1)

        def f_first(m):
            gp.tensor_copy(xc[:, :, :, 0:1].rearrange("p h b l -> p h (b l)"),
                           shift[:, 1, :, bass.ds((m % G) * GB, GB)]).then_inc(s.xc_first, 1)

        def power(m, ve, rstd, ve_sem, done):
            gp.wait_ge(ve_sem, m + 1)
            gp.tensor_tensor(rstd[:], ve[:], neg_half[:], ALU.pow).then_inc(done, 1)

        def p_xf(m, f):
            for half in range(HALF):
                gp.wait_ge(s.mix_scaled, F * HALF * m + f * HALF + half + 1)
                gp.tensor_tensor(xf[:, f, half], xf[:, f, half], xa[:, half, :, 1:L + 1], ALU.add).then_inc(s.xf_ready, 1)

        def w_rs(n, par, q):
            gp.wait_ge(s.state, UNITS * n + q + 1)
            if not (first(n) and q < RING):
                gp.wait_ge(s.reduced, UNITS * n + q - RING + 1)
            gp.tensor_tensor(rs[:, q % RING], rr[:, par, q % HALF], st[:, q % RING], ALU.mult).then_inc(s.rs_prod, 1)

        def body(n, par, p, f, p2):
            for q in range(UNITS):
                w_rs(n, par, q)
                if p is not None and 1 <= q < 6:
                    p_xf(p, q - 1)
                if p2 is not None and q == 13:
                    power(p2, ve, rstd, s.ln1_ve, s.ln1_rstd)
                    p_first(p2)
                if f is not None and q == 6:
                    power(f, ve2, rstd2, s.ln2_ve, s.ln2_rstd)
                    f_first(f)

        gp.wait_ge(s.inits, 5)
        gp.wait_ge(s.consts_in, 64)
        power(0, ve, rstd, s.ln1_ve, s.ln1_rstd)
        p_first(0)
        for f in range(F):
            p_xf(0, f)
        power(1, ve, rstd, s.ln1_ve, s.ln1_rstd)
        p_first(1)
        sweep2(gp, body, ITEMS)
        last = ITEMS - 1
        power(last, ve2, rstd2, s.ln2_ve, s.ln2_rstd)
        f_first(last)

    return block, s


CI = 32
TP = 2
N_TH, N_PH, N_G, N_WZ = 0, TP * CI, 2 * TP * CI, 3 * TP * CI
N_ID = N_WZ + P
N_SAME = N_ID + P
N_VEC = N_SAME + P
N_COLS = N_VEC + 6


def sweep(eng, body, count):
    body(0, 0, 1, None)
    with eng.Fori(0, (count - 2) // 2) as i:
        body(2 * i + 1, 1, 2 * i + 2, 2 * i)
        body(2 * i + 2, 0, 2 * i + 3, 2 * i + 1)
    body(count - 1, 1, None, count - 2)


def nonlocal_phase(nc, ctx, A, xres, kv, sb, sem, psum):
    wn = sb("wn", [P, N_COLS])
    th = sb("th", [TP * CI, 2, 2, C])
    gx = sb("gx", [P, 2, 2, TP * CI])
    pr = sb("pr", [P, 2, TP, 2, C])
    pt = sb("pt", [P, TP, 2, C])
    nm = sb("nm", [P, 2, TP, 2])
    den = sb("den", [P, 2, TP, 2])
    rec = sb("rec", [P, TP, 2])
    yt = sb("yt", [TP * CI, C])
    xs = sb("xs", [P, C])
    wy = sb("wy", [P, NT, C])
    stats = sb("stats", [P, NT // 2, 6])
    mvar = sb("mvar", [P, 2])
    mean = sb("mean", [P, 1])
    dev = sb("dev", [P, 1])
    sqd = sb("sqd", [P, 1])
    ve = sb("nve", [P, 1])
    nh = sb("nh", [P, 1])
    rstd = sb("nrstd", [P, 1])
    scale = sb("nscale", [P, 1])
    shifted = sb("nshifted", [P, 1])
    shift = sb("nshift", [P, 1])
    BT, BG, BY, BZ, BF, BR = psum[0], psum[1], psum[2], psum[3], psum[4:6], psum[6:8]

    names = ("n_w_in kv_in n_theta_prod n_theta n_g_prod n_g n_scores n_negmax n_exp n_recip n_prob n_ptr n_pt_act n_pt_dve n_y_prod n_y "
             "n_z_prod n_z n_bn n_mv n_mean_prod n_mean n_dev n_var_in n_var_prod n_ve n_rstd n_scale n_shift0 "
             "n_shift n_halfs n_affine n_x").split()
    s = type("Sems", (), {n: sem(n) for n in names})
    ident = wn[:, N_ID:N_ID + P]

    def vec(i, n=P):
        return wn[0:n, N_VEC + i:N_VEC + i + 1]

    def tile(buf, t):
        return buf[:, bass.ds(t, 1), :].rearrange("p t c -> p (t c)")

    block = ctx.enter_context(nc.Block())

    @block.sync
    def _(sp):
        sp.dma_start(wn[:], A["wn"]).then_inc(s.n_w_in, 16)
        for part in range(4):
            q = slice(part * NT // 4, (part + 1) * NT // 4)
            sp.dma_start(kv[:, q], A["kv"][:, q]).then_inc(s.kv_in, 16)

    @block.tensor
    def _(pe):
        def a(t):
            if not first(t):
                pe.wait_ge(s.n_theta, t)
                pe.wait_ge(s.n_g, t)
            pe.matmul(BT[0:TP * CI, 0:C], wn[:, N_TH:N_TH + TP * CI], tile(xres, t), start=True, stop=True)
            pe.matmul(BT[0:TP * CI, C:2 * C], wn[:, N_PH:N_PH + TP * CI], tile(kv, t),
                      start=True, stop=True).then_inc(s.n_theta_prod, 1)

        def g(t):
            pe.wait_ge(s.n_x, t + 1)
            for half in range(2):
                m = pe.matmul(BG[:, half * TP * CI:(half + 1) * TP * CI], xs[:, half * P:(half + 1) * P],
                              wn[:, N_G:N_G + TP * CI], start=True, stop=True)
            m.then_inc(s.n_g_prod, 1)

        def scores(t, par):
            pe.wait_ge(s.n_theta, t + 1)
            if not first(t):
                pe.wait_ge(s.n_exp, TP * 2 * t)
            for b in range(TP):
                o = slice(b * CI, (b + 1) * CI)
                for half in range(2):
                    m = pe.matmul(BF[b][:, half * C:(half + 1) * C], th[o, par, 1, half * P:(half + 1) * P],
                                  th[o, par, 0, :], start=True, stop=True)
                m.then_inc(s.n_scores, 1)

        def turn(t, par):
            for b in range(TP):
                pe.wait_ge(s.n_prob, TP * t + b + 1)
                for jh in range(2):
                    for ih in range(2):
                        m = pe.transpose(BR[b][:, jh * C + ih * P:jh * C + (ih + 1) * P],
                                         pr[:, par, b, ih, jh * P:(jh + 1) * P], ident)
                m.then_inc(s.n_ptr, 1)

        def y(t, par):
            pe.wait_ge(s.n_g, t + 1)
            for b in range(TP):
                pe.wait_ge([s.n_pt_act, s.n_pt_dve][b], t + 1)
                for jh in range(2):
                    m = pe.matmul(BY[b * CI:(b + 1) * CI, 0:C], gx[:, par, jh, b * CI:(b + 1) * CI], pt[:, b, jh],
                                  start=jh == 0, stop=jh == 1)
            m.then_inc(s.n_y_prod, 1)

        def wz(t):
            pe.wait_ge(s.n_y, t + 1)
            pe.matmul(BZ[:, 0:C], wn[0:TP * CI, N_WZ:N_WZ + P], yt[:], start=True, stop=True).then_inc(s.n_z_prod, 1)

        def body(t, par, nxt, prev):
            scores(t, par)
            if nxt is not None:
                a(nxt)
                g(nxt)
            if prev is not None:
                turn(prev, 1 - par)
                y(prev, 1 - par)
                wz(prev)

        pe.wait_ge(s.n_w_in, 16)
        pe.wait_ge(s.kv_in, 64)
        a(0)
        g(0)
        sweep(pe, body, NT)
        turn(NT - 1, 1)
        y(NT - 1, 1)
        wz(NT - 1)
        pe.wait_ge(s.n_mv, 1)
        pe.wait_ge(s.n_z, NT)
        pe.matmul(BY[:, 0:1], wn[:, N_SAME:N_SAME + P], mvar[:, 0:1], start=True, stop=True).then_inc(s.n_mean_prod, 1)
        pe.wait_ge(s.n_var_in, 1)
        pe.matmul(BZ[:, 0:1], wn[:, N_SAME:N_SAME + P], sqd[:], start=True, stop=True).then_inc(s.n_var_prod, 1)

    @block.vector
    def _(v):
        def copy_x(t):
            if not first(t):
                v.wait_ge(s.n_g_prod, t)
            v.tensor_copy(xs[:], tile(xres, t)).then_inc(s.n_x, 1)

        def copy_g(t, par):
            v.wait_ge(s.n_g_prod, t + 1)
            v.tensor_copy(gx[:, par].rearrange("p h o -> p (h o)"), BG[:, 0:2 * TP * CI]).then_inc(s.n_g, 1)

        def negmax(t, par):
            for b in range(TP):
                v.wait_ge(s.n_scores, TP * t + b + 1)
                v.tensor_reduce(nm[:, par, b], BF[b][:].rearrange("p (h c) -> p h c", h=2), AX, ALU.max,
                                negate=True).then_inc(s.n_negmax, 1)

        def prob(t, par):
            v.wait_ge(s.n_exp, TP * 2 * (t + 1))
            v.reciprocal(rec[:], den[:, par]).then_inc(s.n_recip, 1)
            v.wait_ge(s.n_recip, t + 1)
            for b in range(TP):
                for half in range(2):
                    m = v.tensor_scalar(pr[:, par, b, half], pr[:, par, b, half], rec[:, b, half:half + 1], None, ALU.mult)
                m.then_inc(s.n_prob, 1)

        def copy_pt(t):
            v.wait_ge(s.n_ptr, TP * t + 2)
            v.tensor_copy(pt[:, 1].rearrange("p j i -> p (j i)"), BR[1][:]).then_inc(s.n_pt_dve, 1)

        def copy_z(t):
            v.wait_ge(s.n_z_prod, t + 1)
            v.tensor_scalar(tile(wy, t), BZ[:, 0:C], vec(3), None, ALU.add).then_inc(s.n_z, 1)

        def body(t, par, nxt, prev):
            if nxt is not None:
                copy_x(nxt)
            negmax(t, par)
            if prev is not None:
                copy_pt(prev)
                copy_z(prev)
            if nxt is not None:
                copy_g(nxt, 1 - par)
            prob(t, par)

        v.memset(nh[:], -0.5).then_inc(s.n_halfs, 1)
        v.wait_ge(s.n_w_in, 16)
        copy_x(0)
        copy_g(0, 0)
        sweep(v, body, NT)
        copy_pt(NT - 1)
        copy_z(NT - 1)
        v.wait_ge(s.n_z, NT)
        for t in range(NT // 2):
            m = v.bn_stats(stats[:, t], wy[:, 2 * t:2 * t + 2].rearrange("p t c -> p (t c)"))
        m.then_inc(s.n_bn, 1)
        v.wait_ge(s.n_bn, 1)
        v.bn_aggr(mvar[:], stats[:].rearrange("p t k -> p (t k)")).then_inc(s.n_mv, 1)
        v.wait_ge(s.n_mean_prod, 1)
        v.tensor_copy(mean[:], BY[:, 0:1]).then_inc(s.n_mean, 1)
        v.wait_ge(s.n_mean, 1)
        v.tensor_tensor(dev[:], mvar[:, 0:1], mean[:], ALU.subtract).then_inc(s.n_dev, 1)
        v.wait_ge(s.n_dev, 1)
        v.scalar_tensor_tensor(out=sqd[:], in0=dev[:], scalar=dev[:, 0:1], in1=mvar[:, 1:2],
                               op0=ALU.mult, op1=ALU.add).then_inc(s.n_var_in, 1)
        v.wait_ge(s.n_var_prod, 1)
        v.tensor_scalar(ve[:], BZ[:, 0:1], EPS, None, ALU.add).then_inc(s.n_ve, 1)
        v.wait_ge(s.n_rstd, 1)
        v.tensor_tensor(scale[:], rstd[:], vec(4), ALU.mult).then_inc(s.n_scale, 1)
        v.wait_ge(s.n_scale, 1)
        v.tensor_tensor(shifted[:], mean[:], scale[:], ALU.mult).then_inc(s.n_shift0, 1)
        v.wait_ge(s.n_shift0, 1)
        v.tensor_tensor(shift[:], vec(5), shifted[:], ALU.subtract).then_inc(s.n_shift, 1)
        for q in range(4):
            v.wait_ge(s.n_affine, q + 1)
            r = slice(q * NT // 4, (q + 1) * NT // 4)
            v.tensor_tensor(xres[:, r].rearrange("p t c -> p (t c)"), xres[:, r].rearrange("p t c -> p (t c)"),
                            wy[:, r].rearrange("p t c -> p (t c)"), ALU.add)

    @block.scalar
    def _(act):
        def theta(t, par):
            act.wait_ge(s.n_theta_prod, t + 1)
            act.activation(th[:, par, 0], BT[0:TP * CI, 0:C], ACT.Identity, bias=vec(0, TP * CI))
            act.activation(th[:, par, 1], BT[0:TP * CI, C:2 * C], ACT.Identity,
                           bias=vec(1, TP * CI)).then_inc(s.n_theta, 1)

        def exps(t, par):
            for b in range(TP):
                act.wait_ge(s.n_negmax, TP * t + b + 1)
                for half in range(2):
                    act.activation(pr[:, par, b, half], BF[b][:, half * C:(half + 1) * C], ACT.Exp,
                                   bias=nm[:, par, b, half:half + 1],
                                   accum_out=den[:, par, b, half:half + 1]).then_inc(s.n_exp, 1)

        def copy_pt(t):
            act.wait_ge(s.n_ptr, TP * t + 1)
            act.copy(pt[:, 0].rearrange("p j i -> p (j i)"), BR[0][:]).then_inc(s.n_pt_act, 1)

        def copy_y(t):
            act.wait_ge(s.n_y_prod, t + 1)
            act.activation(yt[:], BY[0:TP * CI, 0:C], ACT.Identity, bias=vec(2, TP * CI)).then_inc(s.n_y, 1)

        def body(t, par, nxt, prev):
            if nxt is not None:
                theta(nxt, 1 - par)
            exps(t, par)
            if prev is not None:
                copy_pt(prev)
                copy_y(prev)

        act.wait_ge(s.n_w_in, 16)
        theta(0, 0)
        sweep(act, body, NT)
        copy_pt(NT - 1)
        copy_y(NT - 1)
        act.wait_ge(s.n_shift, 1)
        for q in range(4):
            r = slice(q * NT // 4, (q + 1) * NT // 4)
            act.activation(wy[:, r].rearrange("p t c -> p (t c)"), wy[:, r].rearrange("p t c -> p (t c)"), ACT.Identity,
                           bias=shift[:, 0:1], scale=scale[:, 0:1]).then_inc(s.n_affine, 1)

    @block.gpsimd
    def _(gp):
        gp.wait_ge(s.n_halfs, 1)
        gp.wait_ge(s.n_ve, 1)
        gp.tensor_tensor(rstd[:], ve[:], nh[:], ALU.pow).then_inc(s.n_rstd, 1)


A_Q, A_K, A_V, A_O = (i * HALF * C for i in range(4))
A_ID = 4 * HALF * C
A_SEL = A_ID + P
A_VEC = A_SEL + 2 * 16
A_COLS = A_VEC + 7
AT = 2
AB = AT * TP
AN = AT * P
AITEMS = NT // AT
HD = 16


def attention_phase(nc, ctx, A, out, xres, kv, sb, sem, psum):
    wa = sb("wa", [P, A_COLS])
    mk = sb("mk", [P, NT, L], U8)
    mb0 = sb("mb0", [P, NT, L])
    mb = sb("mb", [P, NT, L])
    tgate = sb("tgate", [P, 1])
    nh = sb("anh", [P, AT])
    fence = sb("afence", [P, 1])
    st6 = sb("ast6", [P, AT, 6])
    mv = sb("amv", [P, AT, 2])
    ve = sb("ave", [P, AT])
    rstd = sb("arstd", [P, AT])
    xn = sb("axn", [P, AT, C])
    xs = sb("axs", [P, AT, C])
    at = sb("at", [P, HALF, AB, 2, L])
    xt = sb("xt", [P, HALF, AN])
    qt = sb("qt", [P, 2, HALF, AN])
    km = sb("km", [P, 2, HALF, AB, 2, L])
    vb = sb("vb", [P, 2, AB, 8, 2 * HD])
    e0 = sb("e0", [P, 4, AT, 2, 2, L])
    e = sb("e", [P, 4, AT, 2, 2, L])
    mx = sb("mx", [P, 4, 8])
    den = sb("aden", [P, 4, 8])
    rec = sb("arec", [P, 4, AT, 2, 2])
    pt = sb("apt", [P, 4, AT, 2, P])
    on = sb("on", [P, AT, 2, 4, 2, HD])
    ot = sb("ot", [P, HALF, AN])
    BS, BX, BR = psum[0:4], psum[4:6], psum[6:8]

    names = ("a_w_in a_mask_in a_inits a_mask0 a_mask a_gate a_stats a_ve a_rstd a_xn a_xs a_tr a_at a_xt a_q_prod a_q "
             "a_k_prod a_k a_v_prod a_v a_scores a_masked a_max a_sub a_exp a_den a_rec a_ptr a_pt_act a_pt_dve a_o_prod a_on "
             "a_otr a_ot a_w_prod a_out a_saved").split()
    s = type("Sems", (), {n: sem(n) for n in names})
    ident = wa[:, A_ID:A_ID + P]

    def vec(i):
        return wa[:, A_VEC + i:A_VEC + i + 1]

    def tiles(buf, g, n=AT, t0=0):
        return buf[:, bass.ds(g * AT + t0, n), :]

    block = ctx.enter_context(nc.Block())

    @block.sync
    def _(sp):
        sp.dma_start(wa[:], A["wa"]).then_inc(s.a_w_in, 16)
        for b in range(TP):
            sp.dma_start(mk[b * L:(b + 1) * L], A["mask"][b].unsqueeze(0).broadcast_to([L, NT, L])).then_inc(s.a_mask_in, 16)
        with sp.Fori(0, AITEMS) as g:
            sp.wait_ge(s.a_out, g + 1)
            sp.dma_start(out[:, bass.ds(g * AT, AT), :], tiles(xres, g)).then_inc(s.a_saved, 16)
        sp.wait_ge(s.a_saved, 16 * AITEMS)

    @block.tensor
    def _(pe):
        def p_turn(g):
            for src, bank, ready, freed in ((xn, BX[0], s.a_xn, s.a_v), (xs, BX[1], s.a_xs, s.a_v)):
                pe.wait_ge(ready, g + 1)
                if not first(g):
                    pe.wait_ge(freed, 2 * g)
                for half in range(HALF):
                    for t in range(AT):
                        m = pe.transpose(bank[:, half * AN + t * P:half * AN + (t + 1) * P],
                                         src[:, t, half * P:(half + 1) * P], ident)
                m.then_inc(s.a_tr, 1)

        def p_qk(g):
            pe.wait_ge(s.a_at, HALF * (g + 1))
            pe.wait_ge(s.a_xt, g + 1)
            for off, src, bank, done in ((A_Q, lambda kh: xt[:, kh], BX[0], s.a_q_prod),
                                         (A_K, lambda kh: at[:, kh, :, 0], BX[1], s.a_k_prod)):
                for half in range(HALF):
                    for kh in range(HALF):
                        o = off + kh * C + half * P
                        m = pe.matmul(bank[:, half * AN:(half + 1) * AN], wa[:, o:o + P], src(kh),
                                      start=kh == 0, stop=kh == HALF - 1)
                m.then_inc(done, 1)

        def p_v(g):
            for pair in range(2):
                pe.wait_ge(*((s.a_q, g + 1) if pair == 0 else (s.a_k, 2 * (g + 1))))
                for b in range(2):
                    bb = 2 * pair + b
                    for kh in range(HALF):
                        m = pe.matmul(BX[pair][:, b * C:(b + 1) * C],
                                      at[:, kh, bb].rearrange("p d s -> p (d s)"),
                                      wa[:, A_V + kh * C:A_V + (kh + 1) * C], start=kh == 0, stop=kh == HALF - 1)
                m.then_inc(s.a_v_prod, 1)

        def scores(g, par):
            pe.wait_ge(s.a_k, 2 * (g + 1))
            pe.wait_ge(s.a_q, g + 1)
            if not first(g):
                pe.wait_ge(s.a_masked, 4 * g)
            for t in range(AT):
                for b in range(TP):
                    for half in range(HALF):
                        for q in range(4):
                            r = slice(32 * q, 32 * q + 32)
                            o = (t * 2 + half) * P
                            bb = t * TP + b
                            m = pe.matmul(BS[q][b * L:(b + 1) * L, o:o + P], qt[r, par, half, bb * L:(bb + 1) * L],
                                          km[r, par, half, bb].rearrange("p m s -> p (m s)"), start=True, stop=True)
            m.then_inc(s.a_scores, 1)

        def turn(g, q):
            pe.wait_ge(s.a_exp, 4 * g + q + 1)
            if q >= 2:
                pe.wait_ge(*((s.a_pt_dve, 3 * g + 1) if q == 2 else (s.a_pt_act, g + 1)))
            elif not first(g):
                pe.wait_ge(s.a_out if q == 0 else s.a_ot, g)
            for t in range(AT):
                for half in range(HALF):
                    m = pe.transpose(BR[q % 2][:, (t * 2 + half) * P:(t * 2 + half + 1) * P],
                                     e[:, q, t, half].rearrange("p m s -> p (m s)"), ident)
            m.then_inc(s.a_ptr, 1)

        def values(g, par):
            pe.wait_ge(s.a_v, 2 * (g + 1))
            pe.wait_ge(s.a_pt_dve, 3 * (g + 1))
            pe.wait_ge(s.a_pt_act, g + 1)
            for t in range(AT):
                for b in range(TP):
                    for half in range(HALF):
                        for q in range(4):
                            o = t * C + half * P + q * 2 * HD
                            m = pe.matmul(BR[0][b * L:(b + 1) * L, o:o + 2 * HD], pt[:, q, t, half, b * L:(b + 1) * L],
                                          vb[:, par, t * TP + b, half * 4 + q], start=True, stop=True)
            m.then_inc(s.a_o_prod, 1)

        def output(g):
            pe.wait_ge(s.a_on, g + 1)
            for half in range(HALF):
                for t in range(AT):
                    m = pe.transpose(BR[1][:, half * AN + t * P:half * AN + (t + 1) * P],
                                     on[:, t, half].rearrange("p q m d -> p (q m d)"), ident)
            m.then_inc(s.a_otr, 1)
            pe.wait_ge(s.a_ot, g + 1)
            for t in range(AT):
                for kh in range(HALF):
                    m = pe.matmul(BR[0][:, t * C:(t + 1) * C], ot[:, kh, t * P:(t + 1) * P],
                                  wa[:, A_O + kh * C:A_O + (kh + 1) * C], start=kh == 0, stop=kh == HALF - 1)
            m.then_inc(s.a_w_prod, 1)

        def body(g, par, nxt, prev):
            if nxt is not None:
                p_turn(nxt)
                p_qk(nxt)
            turn(g, 0)
            turn(g, 1)
            if nxt is not None:
                p_v(nxt)
            turn(g, 2)
            turn(g, 3)
            values(g, par)
            if nxt is not None:
                scores(nxt, 1 - par)
            output(g)

        pe.wait_ge(s.a_w_in, 16)
        p_turn(0)
        p_qk(0)
        p_v(0)
        scores(0, 0)
        sweep(pe, body, AITEMS)

    @block.vector
    def _(v):
        def p_norm(g):
            v.memset(fence[:], 0.0)
            for t in range(AT):
                v.bn_stats(st6[:, t], tiles(kv, g, 1, t).rearrange("p t c -> p (t c)")).then_inc(s.a_stats, 1)
            v.wait_ge(s.a_stats, 2 * AT * g + AT)
            v.memset(fence[:], 0.0)
            for t in range(AT):
                v.bn_aggr(mv[:, t], st6[:, t]).then_inc(s.a_stats, 1)
            v.wait_ge(s.a_stats, 2 * AT * (g + 1))
            v.tensor_scalar(ve[:], mv[:, :, 1], EPS, None, ALU.add).then_inc(s.a_ve, 1)
            if not first(g):
                v.wait_ge(s.a_tr, 2 * g)
            v.tensor_copy(xs[:], tiles(xres, g)).then_inc(s.a_xs, 1)
            v.wait_ge(s.a_rstd, g + 1)
            for t in range(AT):
                m = v.tensor_scalar(xn[:, t], tiles(kv, g, 1, t).rearrange("p t c -> p (t c)"),
                                    mv[:, t, 0:1], rstd[:, t:t + 1], ALU.subtract, ALU.mult)
            m.then_inc(s.a_xn, 1)

        def p_xt(g):
            v.wait_ge(s.a_tr, 2 * (g + 1))
            v.tensor_copy(xt[:].rearrange("p h n -> p (h n)"), BX[1][:]).then_inc(s.a_xt, 1)

        def p_v(g, par):
            for pair in range(2):
                v.wait_ge(s.a_v_prod, 2 * g + pair + 1)
                v.tensor_tensor(vb[:, par, 2 * pair:2 * pair + 2].rearrange("p b q c -> p (b q) c"),
                                BX[pair][:].rearrange("p (x c) -> p x c", c=2 * HD),
                                wa[:, A_SEL:A_SEL + 2 * HD].unsqueeze(1).broadcast_to([P, 16, 2 * HD]),
                                ALU.mult).then_inc(s.a_v, 1)

        def mask_scores(g):
            v.wait_ge(s.a_scores, g + 1)
            for q in range(4):
                for t in range(AT):
                    m = v.tensor_tensor(e0[:, q, t].rearrange("p h m s -> p (h m) s"),
                                        BS[q][:, t * C:(t + 1) * C].rearrange("p (x s) -> p x s", s=L),
                                        mb[:, bass.ds(g * AT + t, 1), :].broadcast_to([P, 4, L]), ALU.add)
                m.then_inc(s.a_masked, 1)
            for q in range(4):
                v.wait_ge(s.a_masked, 4 * g + q + 1)
                v.tensor_reduce(mx[:, q], e0[:, q].rearrange("p t h m s -> p (t h m) s"), AX, ALU.max).then_inc(s.a_max, 1)

        def sums(g):
            for q in range(4):
                v.wait_ge(s.a_exp, 4 * g + q + 1)
                v.tensor_reduce(den[:, q], e[:, q].rearrange("p t h m s -> p (t h m) s"), AX, ALU.add).then_inc(s.a_den, 1)
            v.wait_ge(s.a_den, 4 * (g + 1))
            v.reciprocal(rec[:].rearrange("p q t h m -> p q (t h m)"), den[:]).then_inc(s.a_rec, 1)

        def copy_pt(g, q):
            v.wait_ge(s.a_ptr, 4 * g + q + 1)
            v.tensor_copy(pt[:, q].rearrange("p t h x -> p (t h x)"), BR[q % 2][:]).then_inc(s.a_pt_dve, 1)

        def norm(g):
            v.wait_ge(s.a_o_prod, g + 1)
            v.wait_ge(s.a_rec, g + 1)
            for t in range(AT):
                for half in range(HALF):
                    o = t * C + half * P
                    m = v.tensor_tensor(on[:, t, half], BR[0][:, o:o + P].rearrange("p (q m d) -> p q m d", q=4, m=2),
                                        rec[:, :, t, half].unsqueeze(3).broadcast_to([P, 4, 2, HD]), ALU.mult)
            m.then_inc(s.a_on, 1)

        def result(g):
            v.wait_ge(s.a_w_prod, g + 1)
            v.scalar_tensor_tensor(out=tiles(xres, g).rearrange("p t c -> p (t c)"), in0=BR[0][:], scalar=tgate[:, 0:1],
                                   in1=tiles(xres, g).rearrange("p t c -> p (t c)"), op0=ALU.mult,
                                   op1=ALU.add).then_inc(s.a_out, 1)

        def body(g, par, nxt, prev):
            if nxt is not None:
                p_norm(nxt)
                p_xt(nxt)
            copy_pt(g, 0)
            sums(g)
            if nxt is not None:
                p_v(nxt, 1 - par)
            copy_pt(g, 2)
            copy_pt(g, 3)
            norm(g)
            if nxt is not None:
                mask_scores(nxt)
            result(g)

        v.memset(nh[:], -0.5).then_inc(s.a_inits, 1)
        v.wait_ge(s.a_mask_in, 32)
        v.tensor_scalar(mb0[:], mk[:], -1.0, 3e38, ALU.add, ALU.mult).then_inc(s.a_mask0, 1)
        v.wait_ge(s.a_mask0, 1)
        v.tensor_scalar(mb[:], mb0[:], 10.0, None, ALU.mult).then_inc(s.a_mask, 1)
        v.wait_ge(s.a_mask, 1)
        v.wait_ge(s.a_w_in, 16)
        v.wait_ge(s.a_gate, 1)
        p_norm(0)
        p_xt(0)
        p_v(0, 0)
        mask_scores(0)
        sweep(v, body, AITEMS)

    @block.scalar
    def _(act):
        def p_at(g):
            act.wait_ge(s.a_tr, 2 * g + 1)
            for half in range(HALF):
                act.activation(at[:, half], BX[0][:, half * AN:(half + 1) * AN].rearrange("p (b s) -> p b s", s=L)
                               .unsqueeze(2).broadcast_to([P, AB, 2, L]), ACT.Identity,
                               bias=vec(2 + half), scale=vec(half)).then_inc(s.a_at, 1)

        def p_qk(g, par):
            act.wait_ge(s.a_q_prod, g + 1)
            act.activation(qt[:, par].rearrange("p h n -> p (h n)"), BX[0][:], ACT.Copy, scale=HD ** -0.5).then_inc(s.a_q, 1)
            act.wait_ge(s.a_k_prod, g + 1)
            for m in range(2):
                act.activation(km[:, par, :, :, m].rearrange("p h b s -> p (h b) s"),
                               BX[1][:].rearrange("p (x s) -> p x s", s=L), ACT.Copy, scale=vec(4 + m)).then_inc(s.a_k, 1)

        def exps(g, q):
            act.wait_ge(s.a_sub, 4 * g + q + 1)
            act.activation(e[:, q].rearrange("p t h m s -> p (t h m s)"), e0[:, q].rearrange("p t h m s -> p (t h m s)"),
                           ACT.Exp).then_inc(s.a_exp, 1)

        def copy_pt(g):
            act.wait_ge(s.a_ptr, 4 * g + 2)
            act.copy(pt[:, 1].rearrange("p t h x -> p (t h x)"), BR[1][:]).then_inc(s.a_pt_act, 1)

        def copy_ot(g):
            act.wait_ge(s.a_otr, g + 1)
            act.copy(ot[:].rearrange("p h n -> p (h n)"), BR[1][:]).then_inc(s.a_ot, 1)

        def body(g, par, nxt, prev):
            exps(g, 0)
            exps(g, 1)
            if nxt is not None:
                p_at(nxt)
                p_qk(nxt, 1 - par)
            exps(g, 2)
            exps(g, 3)
            copy_pt(g)
            copy_ot(g)

        act.wait_ge(s.a_w_in, 16)
        act.activation(tgate[:], vec(6), ACT.Tanh).then_inc(s.a_gate, 1)
        p_at(0)
        p_qk(0, 0)
        sweep(act, body, AITEMS)

    @block.gpsimd
    def _(gp):
        def power(g):
            gp.wait_ge(s.a_ve, g + 1)
            gp.tensor_tensor(rstd[:], ve[:], nh[:], ALU.pow).then_inc(s.a_rstd, 1)

        def subs(g):
            for q in range(4):
                gp.wait_ge(s.a_max, 4 * g + q + 1)
                x = e0[:, q].rearrange("p t h m s -> p (t h m) s")
                gp.tensor_tensor(x, x, mx[:, q].unsqueeze(2).broadcast_to([P, 8, L]), ALU.subtract).then_inc(s.a_sub, 1)

        def body(g, par, nxt, prev):
            subs(g)
            if nxt is not None:
                power(nxt)

        gp.wait_ge(s.a_inits, 1)
        power(0)
        sweep(gp, body, AITEMS)


def constants():
    import numpy as np
    h, i = np.arange(P) // S, np.arange(P) % S
    same = (h[:, None] == h[None, :]).astype(np.float32)
    c, rep = np.zeros((P, C_COLS), np.float32), np.zeros((P, S * P), np.float32)
    for j in range(S):
        rep[:, j * P:(j + 1) * P] = same * (i[:, None] == j)
        c[:, C_RED + j * P:C_RED + (j + 1) * P] = same * ((i[None, :] == j) - 1.0 / S)
    c[:, C_CEN:C_CEN + P] = same * ((i[:, None] == i[None, :]) - 1.0 / S)
    c[:, C_ONE:C_ONE + P] = same
    c[:, C_ID:C_ID + P] = np.eye(P)
    c[:, C_AVG:C_AVG + P // S] = (h[:, None] == np.arange(P // S)[None, :]) / S
    return c, rep


def build(nc, A, out):
    with ExitStack() as ctx:
        def sb(name, shape, dt=F32):
            return ctx.enter_context(nc.sbuf_tensor(name, shape, dt))

        def sem(name):
            return ctx.enter_context(nc.semaphore(name))

        psum = [ctx.enter_context(nc.psum_tensor(f"bank{i}", [P, N], F32)) for i in range(8)]
        xres = sb("xres", [P, NT, C])
        with ExitStack() as inner:
            def sb1(name, shape, dt=F32):
                return inner.enter_context(nc.sbuf_tensor(name, shape, dt))

            def sem1(name):
                return inner.enter_context(nc.semaphore(name))

            rwkv_phase(nc, inner, A, xres, sb1, sem1, psum)
        kv = sb("kv", [P, NT, C])
        for phase, outs in ((nonlocal_phase, ()), (attention_phase, (out,))):
            with ExitStack() as inner:
                def sb2(name, shape, dt=F32):
                    return inner.enter_context(nc.sbuf_tensor(name, shape, dt))

                def sem2(name):
                    return inner.enter_context(nc.semaphore(name))

                phase(nc, inner, A, *outs, xres, kv, sb2, sem2, psum)


def layouts(np, I):
    def halves(w):
        return w.reshape(HALF, P, -1).transpose(1, 0, 2).reshape(P, -1)

    def col(v):
        return v.reshape(HALF, P).T

    def pad(a):
        return np.concatenate([a, np.zeros((P - a.shape[0],) + a.shape[1:], a.dtype)], 0)

    wps, wfs = [], []
    for l in range(2):
        g = lambda n: np.asarray(I[f"L{l}_xattn_{n}"])
        order = [0, 1, 2, 3, 4] if l == 0 else [1, 0, 2, 3, 4]
        w1 = g("maa_w1").reshape(C, F, DM)[:, order].reshape(C, F * DM)
        w2 = g("maa_w2")[order]
        maa = ([g("maa_" + n) for n in "wkvrg"] if l == 0 else list(g("maa_stack")[0][order]))
        d1, d2, u = (g("decay_w1"), g("decay_w2"), g("faaaa")) if l == 0 else (g("td_w1"), g("td_w2"), g("u"))
        wps.append(np.concatenate(
            [halves(w1), halves(d1)] + [halves(g(n).T) for n in ("Wk", "Wv", "Wr", "Wg")]
            + [w2[:4].reshape(4 * DM, C), pad(w2[4]), pad(d2)]
            + [col(v) for v in [g("ln1_w"), g("ln1_b"), g("maa_x")] + maa + [g("time_decay"), u.reshape(C)]], 1))
        fk, fr, wk, wr, wv = (("fmaa_k", "fmaa_r", "fWk", "fWr", "fWv") if l == 0 else
                              ("ffn_maa_k", "ffn_maa_r", "Wfk", "Wfr", "Wfv"))
        wfs.append(np.concatenate(
            [halves(g(n).T) for n in ("Wo", wk, wr, wv)]
            + [col(g(n)) for n in ("ln2_w", "ln2_b", "gn_w", "gn_b", fk, fr)], 1))
    ctx = np.asarray(I["ctx_2048"])
    tok = lambda a: np.ascontiguousarray(a.reshape(NT, P, C).transpose(1, 0, 2))
    s0 = ctx[:, 2:2 + S].reshape(B, HALF, P, S).transpose(2, 1, 3, 0)
    shift = np.stack([ctx[:, 1], ctx[:, 0]]).reshape(2, B, HALF, P).transpose(3, 0, 2, 1)
    g = lambda n: np.asarray(I["L2_xattn_" + n])

    def twice(w):
        z = np.zeros_like(w)
        return np.concatenate([np.concatenate([w, z], 1), np.concatenate([z, w], 1)], 0)

    two = lambda v: pad(np.tile(v, 2)[:, None])
    row = np.arange(P)
    wn = np.concatenate(
        [twice(g(n).T) for n in ("Wtheta", "Wphi", "Wg")] + [pad(twice(g("Wz").T)), np.eye(P, dtype=np.float32),
         (row[:, None] % L == row[None, :] % L).astype(np.float32) / 2]
        + [two(g(n)) for n in ("btheta", "bphi", "bg", "bz", "gamma", "beta")], 1)
    g = lambda n: np.asarray(I["L3_xattn_" + n])
    parity = np.stack([row // HD % 2 == 0, row // HD % 2 == 1], 1).astype(np.float32)
    wa = np.concatenate(
        [halves(g(n).T) for n in ("Wq", "Wk", "Wv", "Wo")]
        + [np.eye(P, dtype=np.float32), (row[:, None] // L == np.arange(2 * HD)[None, :] // HD).astype(np.float32),
           col(g("ln_gamma")), col(g("ln_beta")), parity, np.tile(g("gate")[None], (P, 1))], 1)
    mask = np.asarray(I["mask_BxS2_bf1"]).view(np.uint8).reshape(NT, TP, L).transpose(1, 0, 2)
    return {"wn": wn, "wa": wa, "kv": tok(ctx), "mask": mask, "x": tok(np.asarray(I["x"])), "wp": np.stack(wps), "wf": np.stack(wfs), "cst": constants()[0], "rep": constants()[1],
            "s0": s0, "shift": shift}


def kernel(**inputs):
    import numpy as np
    import concourse.bacc as bacc
    from concourse.bass_utils import run_bass_kernel_spmd as run

    nc = bacc.Bacc("TRN2", target_bir_lowering=False, num_devices=1)
    arrays = {k: np.ascontiguousarray(v) for k, v in layouts(np, inputs).items()}
    A = {k: nc.dram_tensor(k + "_dram", v.shape, mybir.dt.from_np(v.dtype), kind="ExternalInput").ap() for k, v in arrays.items()}
    out = nc.dram_tensor("out_dram", (P, NT, C), F32, kind="ExternalOutput").ap()
    build(nc, A, out)
    r = run(nc, [{k + "_dram": v for k, v in arrays.items()}], core_ids=[0])
    return r.results[0]["out_dram"].reshape(P, NT, C).transpose(1, 0, 2).reshape(B, L, C)
```
